# Optimizing a Trainium2 kernel written in Bass

```python
import numpy as np
import jax
import jax.numpy as jnp

def _softmax(x, axis=-1):
    return jax.nn.softmax(x, axis=axis)

def _gelu(x):
    return jax.nn.gelu(x, approximate=True)

def _silu(x):
    return jax.nn.silu(x)

def _sigmoid(x):
    return jax.nn.sigmoid(x)

def _layernorm(x, axis=-1, eps=1e-05):
    m = jnp.mean(x, axis=axis, keepdims=True)
    v = jnp.var(x, axis=axis, keepdims=True)
    return (x - m) / jnp.sqrt(v + eps)

def _scatter_add(tgt, idx, src, axis=0):
    return tgt.at[idx].add(src)

def _segment_sum(src, seg, n):
    return jax.ops.segment_sum(src, seg, n)
kernel_name = 'mk_seq_postln_d1_jaxref_r2_9bd3cb'

def setup_inputs(seed: int=0):
    np.random.seed(seed)
    _w = jnp.asarray

    def _L0_attn_setup():
        import jax, jax.numpy as jnp
        import numpy as np
        B, L, D, H, K = (4, 1024, 512, 16, 3)
        HEAD_DIM = D // H
        LN_EPS = 1e-05
        key = jax.random.key(seed)
        ks = jax.random.split(key, 12)
        w = lambda k, shp: jax.random.normal(k, shp, jnp.float32) * shp[-1] ** (-0.5)
        return {'x': jax.random.normal(ks[0], (B, L, D), jnp.float32), 'band_importance': jax.random.normal(ks[1], (1, L), jnp.float32) * 0.02, 'Wq': w(ks[2], (D, D)), 'bq': jnp.zeros((D,), jnp.float32), 'Wk': w(ks[3], (D, D)), 'bk': jnp.zeros((D,), jnp.float32), 'Wv': w(ks[4], (D, D)), 'bv': jnp.zeros((D,), jnp.float32), 'Wo': w(ks[5], (D, D)), 'bo': jnp.zeros((D,), jnp.float32), 'gamma': jnp.ones((D,), jnp.float32), 'beta': jnp.zeros((D,), jnp.float32)}
    _L0_attn_in = _L0_attn_setup()

    def _L0_ffn_setup():
        import jax, jax.numpy as jnp
        import numpy as np
        IN_FEATURES = 512
        ACT_BITS = 4

        def _hadamard(size: int) -> np.ndarray:
            h = np.array([[1.0]], dtype=np.float64)
            while h.shape[0] < size:
                h = np.block([[h, h], [h, -h]])
            return (h / np.sqrt(size)).astype(np.float32)

        def _quantize_activations(x, bits=ACT_BITS):
            pos = 2 ** (bits - 1) - 1
            neg = 2 ** (bits - 1)
            scale = jnp.clip(jnp.max(jnp.abs(jax.lax.stop_gradient(x)), axis=-1, keepdims=True), 1e-05) / pos
            q = jnp.clip(jnp.round(x / scale), -neg, pos) * scale
            return x + jax.lax.stop_gradient(q - x)

        def _ternary_quantize_ste(w):
            scale = jnp.clip(jnp.mean(jnp.abs(jax.lax.stop_gradient(w)), axis=1, keepdims=True), 1e-05)
            n = w / scale
            tern = jnp.where(n > 0.5, 1.0, jnp.where(n < -0.5, -1.0, 0.0))
            q = tern * scale
            return w + jax.lax.stop_gradient(q - w)
        key = jax.random.key(seed)
        k1, k2 = jax.random.split(key)
        x = jax.random.normal(k1, (8, 4096, IN_FEATURES), dtype=jnp.float32)
        bound = 1.0 / np.sqrt(IN_FEATURES)
        weight = jax.random.uniform(k2, (512, IN_FEATURES), dtype=jnp.float32, minval=-bound, maxval=bound)
        return {'x': x, 'weight': weight}
    _L0_ffn_in = _L0_ffn_setup()
    _d = {'L0_attn_x': _L0_attn_in['x'], 'L0_attn_band_importance': _L0_attn_in['band_importance'], 'L0_attn_Wq': _L0_attn_in['Wq'], 'L0_attn_bq': _L0_attn_in['bq'], 'L0_attn_Wk': _L0_attn_in['Wk'], 'L0_attn_bk': _L0_attn_in['bk'], 'L0_attn_Wv': _L0_attn_in['Wv'], 'L0_attn_bv': _L0_attn_in['bv'], 'L0_attn_Wo': _L0_attn_in['Wo'], 'L0_attn_bo': _L0_attn_in['bo'], 'L0_attn_gamma': _L0_attn_in['gamma'], 'L0_attn_beta': _L0_attn_in['beta'], 'L0_ffn_weight': _L0_ffn_in['weight']}
    _x0 = _d['L0_attn_x']
    _d['L0_attn_x'] = jax.random.normal(jax.random.fold_in(jax.random.key(seed), 1), (4, 2048, 512), dtype=_x0.dtype)
    del _x0
    return _d

def reference(L0_attn_x, L0_attn_band_importance, L0_attn_Wq, L0_attn_bq, L0_attn_Wk, L0_attn_bk, L0_attn_Wv, L0_attn_bv, L0_attn_Wo, L0_attn_bo, L0_attn_gamma, L0_attn_beta, L0_ffn_weight):

    def _L0_attn_ref(x, band_importance, Wq, bq, Wk, bk, Wv, bv, Wo, bo, gamma, beta):
        import jax, jax.numpy as jnp
        import numpy as np
        B, L, D, H, K = (4, 1024, 512, 16, 3)
        HEAD_DIM = D // H
        LN_EPS = 1e-05
        Bx, Lx, Dx = x.shape
        hd = Dx // H
        imp = jax.nn.softmax(band_importance, axis=-1)[0]
        _, idx = jax.lax.top_k(imp, K)
        col_mask = jnp.zeros((Lx,), bool).at[idx].set(True)
        bias = jnp.where(col_mask, -jnp.inf, 0.0).astype(x.dtype)
        q = (x @ Wq.T + bq).reshape(Bx, Lx, H, hd)
        k_ = (x @ Wk.T + bk).reshape(Bx, Lx, H, hd)
        v = (x @ Wv.T + bv).reshape(Bx, Lx, H, hd)
        scale = 1.0 / np.sqrt(hd)
        scores = jnp.einsum('bqhd,bkhd->bhqk', q, k_) * scale + bias[None, None, None, :]
        attn = jax.nn.softmax(scores, axis=-1)
        ctx = jnp.einsum('bhqk,bkhd->bqhd', attn, v).reshape(Bx, Lx, Dx)
        attn_out = ctx @ Wo.T + bo
        y = x + attn_out
        mu = jnp.mean(y, axis=-1, keepdims=True)
        var = jnp.mean((y - mu) ** 2, axis=-1, keepdims=True)
        return (y - mu) * jax.lax.rsqrt(var + LN_EPS) * gamma + beta

    def _L0_ffn_ref(x, weight):
        import jax, jax.numpy as jnp
        import numpy as np
        IN_FEATURES = 512
        ACT_BITS = 4

        def _hadamard(size: int) -> np.ndarray:
            h = np.array([[1.0]], dtype=np.float64)
            while h.shape[0] < size:
                h = np.block([[h, h], [h, -h]])
            return (h / np.sqrt(size)).astype(np.float32)

        def _quantize_activations(x, bits=ACT_BITS):
            pos = 2 ** (bits - 1) - 1
            neg = 2 ** (bits - 1)
            scale = jnp.clip(jnp.max(jnp.abs(jax.lax.stop_gradient(x)), axis=-1, keepdims=True), 1e-05) / pos
            q = jnp.clip(jnp.round(x / scale), -neg, pos) * scale
            return x + jax.lax.stop_gradient(q - x)

        def _ternary_quantize_ste(w):
            scale = jnp.clip(jnp.mean(jnp.abs(jax.lax.stop_gradient(w)), axis=1, keepdims=True), 1e-05)
            n = w / scale
            tern = jnp.where(n > 0.5, 1.0, jnp.where(n < -0.5, -1.0, 0.0))
            q = tern * scale
            return w + jax.lax.stop_gradient(q - w)
        H = jnp.asarray(_hadamard(IN_FEATURES))
        xh = x @ H
        xq = _quantize_activations(xh)
        wq = _ternary_quantize_ste(weight)
        return jnp.einsum('bsi,oi->bso', xq, wq)
    x = L0_attn_x
    x = _layernorm(x + _L0_attn_ref(x, L0_attn_band_importance, L0_attn_Wq, L0_attn_bq, L0_attn_Wk, L0_attn_bk, L0_attn_Wv, L0_attn_bv, L0_attn_Wo, L0_attn_bo, L0_attn_gamma, L0_attn_beta), axis=-1)
    x = _layernorm(x + _L0_ffn_ref(x, L0_ffn_weight), axis=-1)
    return x

_drawn_inputs = setup_inputs


def setup_inputs(seed=0):
    import zlib

    import numpy as np

    out = dict(_drawn_inputs(seed))
    spreads = {'L0_attn_bq': (0.0, 0.597),
     'L0_attn_bk': (0.0, 0.8),
     'L0_attn_bv': (0.0, 0.1),
     'L0_attn_bo': (0.0, 0.1),
     'L0_attn_gamma': (1.0, 0.2),
     'L0_attn_beta': (0.0, 0.1)}
    factors = {'L0_attn_band_importance': 8.0}
    for name, (base, spread) in spreads.items():
        noise = np.random.default_rng([zlib.crc32(name.encode()), seed]).standard_normal(out[name].shape)
        drawn = base * np.exp(spread * noise) if base else spread * noise
        out[name] = jnp.asarray(drawn.astype(out[name].dtype))
    for name, factor in factors.items():
        out[name] = (out[name] * factor).astype(out[name].dtype)
    return out
```

```python
from contextlib import ExitStack

import numpy as np

import concourse.bass as bass
from concourse import mybir

ALU = mybir.AluOpType
ACT = mybir.ActivationFunctionType
AX = mybir.AxisListType
F32 = mybir.dt.float32
F32R = mybir.dt.float32r
BF16 = mybir.dt.bfloat16

P = 128
NB, L, D = 4, 2048, 512
NH, HD = 16, 32
LBAND = 1024
TOPK = 3
HG = 4
NG = NH // HG
NS = NB * NG
IC = D // P
QB = 512
NQB = L // QB
NKC = L // P
UNITS = HG * (QB // P) * NQB
SCALE = 1.0 / float(np.sqrt(HD))
LN_EPS = 1e-5
MASKED = -2.0 ** 80
MAGIC = 1.5 * 2.0 ** 23
RMASK, RM0, RSTACK, RALL = 96, 97, 97, 99
PAD, FOUND = -5.0, -7.0
NSTK = 3 * 16

POOL_CHUNKS = [0, 1, 2, 4, 5, 7, 8, 10, 11]
NADD = len(POOL_CHUNKS) - 1
ADD_OF = {c: max(i - 1, 0) for i, c in enumerate(POOL_CHUNKS)}
PE_FIRST = next(c for c in range(NKC) if c not in POOL_CHUNKS)
FIRST_UNITS = 2
TPG = 4
NGRP = L // P // TPG
C_DVE = 65


def unit_steps():
    places = [(c, i) for c in range(FIRST_UNITS, NKC) for i in (0, 1, 1, 2, 2, 3) if i < 3 or c not in POOL_CHUNKS]
    steps = {}
    for u in range(UNITS):
        steps.setdefault(places[u * len(places) // UNITS], []).append(u)
    return steps


def wait_alone(eng, sem, value, passed):
    eng.wait_ge(sem, value)
    eng.sem_inc(passed, 1)


def build(nc, x, xT, wT, bqkv, woT, w_ffn, band, gamma, beta, bo, had, out):
    units_at = unit_steps()
    ctxT = nc.dram_tensor("ctxT_dram", (NS, P, L), F32, kind="Internal").ap()

    with ExitStack() as ctx:
        def sb(name, shape, dt=F32):
            return ctx.enter_context(nc.sbuf_tensor(name, shape, dt))

        def sem(name):
            return ctx.enter_context(nc.semaphore(name))

        kst = [sb(f"kst{i}", [P, HG, L], F32R) for i in range(2)]
        qcur = sb("qcur", [P, NQB, HG, QB], F32R)
        qnew = sb("qnew", [P, HG, QB], F32R)
        vst = sb("vst", [P, 2, NKC, P])
        prob = sb("prob", [P, 3, HG, QB])
        acc = sb("acc", [P, HG, QB])
        xk = sb("xk", [P, 2, IC, QB])
        xq = sb("xq", [P, IC, QB])
        wkv = sb("wkv", [P, 2, IC, P])
        wq = sb("wq", [P, IC, P])
        bias = sb("bias", [P, 3 * NG])
        hi = sb("hi", [P, 2, QB], F32R)
        lo = sb("lo", [P, 2, QB], F32R)
        umax = sb("umax", [P, UNITS // NQB, NQB])
        negm = sb("negm", [P, HG * NQB])
        msplit = sb("msplit", [P, 2 * HG * NQB])
        mhi = sb("mhi", [P, HG * NQB], F32R)
        mrow = sb("mrow", [2 * HG * NQB, P], F32R)
        ident = sb("ident", [P, P])
        identb = sb("identb", [P, P], BF16)
        ones = sb("ones", [P, P])
        hadm = sb("hadm", [P, P])
        ternT = sb("ternT", [P, IC, D], BF16)
        wscale = sb("wscale", [P, D])
        small = sb("small", [P, 64])
        band_buf = vst[0:1].rearrange("p a c d -> p (a c d)")[:, 0:2 * (LBAND + 8)].rearrange("p (a n) -> p a n", a=2)
        stats = sb("stats", [P, TPG, 6])
        mv = sb("mv", [P, TPG, 2])
        lnv = sb("lnv", [P, TPG, 4])
        qsc = sb("qsc", [P, TPG, 4])

        rows = prob[:].rearrange("p a b c -> p (a b) c")
        tA = [rows[:, 3 * t, :] for t in range(4)]
        tB = [rows[:, 3 * t + 1, :] for t in range(4)]
        tC = [rows[:, 3 * t + 2, :] for t in range(4)]
        wo_sb = vst[:, 1].rearrange("p c d -> p (c d)").rearrange("p (g n) -> p g n", g=IC)
        gam, bet, bob = acc[:, 0, :], acc[:, 1, :], acc[:, 2, :]

        ps_s = ctx.enter_context(nc.psum_tensor("ps_s", [P, HG, QB], F32))
        ps_o = ctx.enter_context(nc.psum_tensor("ps_o", [P, QB], F32))
        ps_z = ctx.enter_context(nc.psum_tensor("ps_z", [P, QB], F32))
        ps_m = ctx.enter_context(nc.psum_tensor("ps_m", [P, 2, QB], F32))
        bank2 = [ps_o[:, :], ps_z[:, :], ps_m[:, 0, :], ps_m[:, 1, :]]


        wf = rows[:, 0:4, :]
        ternb = rows[:, 4:6, :].rearrange("p a n -> p (a n)").bitcast(BF16).rearrange("p (c n) -> p c n", c=IC)
        neg, diag = rows[:, 6, :], rows[:, 7, :]
        band_row = rows[0:1, 8:10, :].rearrange("p a n -> p (a n)")
        band_all = band_buf[0:1, 0, :]
        band_e, band_e_pad = band_all[:, 0:LBAND], band_all[:, LBAND:]
        band_all2 = band_buf[0:1, 1, :]
        band_s = small[0:1, 16:32]
        qmask = qnew[0:1].rearrange("p h x -> p (h x)")

        passed = sem("passed")
        band_ld = sem("band_ld")
        wf_ld = sem("wf_ld")
        had_ld = sem("had_ld")
        bias_ld = sem("bias_ld")
        mask_ld = sem("mask_ld")
        wkv_ld = sem("wkv_ld")
        wq_ld = sem("wq_ld")
        xq_ld = sem("xq_ld")
        q_stk = sem("q_stk")
        q_cur = sem("q_cur")
        cst = sem("cst")
        c_par = sem("c_par")
        c_st = sem("c_st")
        stk_ones = sem("stk_ones")
        idf = sem("idf")
        mask_ok = sem("mask_ok")
        band_mx = sem("band_mx")
        band_ex = sem("band_ex")
        dstep = sem("dstep")
        tern_ok = sem("tern_ok")
        tern_t = sem("tern_t")
        tern_c = sem("tern_c")
        kproj = sem("kproj")
        vproj = sem("vproj")
        qproj = sem("qproj")
        k_hi = sem("k_hi")
        k_lo = sem("k_lo")
        v_cp = sem("v_cp")
        q_hi = sem("q_hi")
        q_lo = sem("q_lo")
        msc = sem("msc")
        mred = sem("mred")
        mstep = sem("mstep")
        mneg = sem("mneg")
        mtr = sem("mtr")
        mcp = sem("mcp")
        sc = sem("sc")
        ex = sem("ex")
        pv = sem("pv")
        padd = sem("padd")
        zdone = sem("zdone")
        zinv = sem("zinv")
        cnorm = sem("cnorm")
        cbias = sem("cbias")
        c_xb = sem("c_xb")
        c_xg = sem("c_xg")
        c_wo = sem("c_wo")
        c_ve = sem("c_ve")
        c_sd = sem("c_sd")
        c_n1 = sem("c_n1")
        c_ng = sem("c_ng")
        c_x1 = sem("c_x1")
        c_w = sem("c_w")
        c_ws = sem("c_ws")
        c_wt = sem("c_wt")
        c_wtc = sem("c_wtc")
        c_h = sem("c_h")
        c_q1 = sem("c_q1")
        c_q = sem("c_q")
        c_qt = sem("c_qt")
        c_qtc = sem("c_qtc")
        c_ffn = sem("c_ffn")
        c_o = sem("c_o")
        c_dve = sem("c_dve")
        k_stk = [sem("k_stk0"), sem("k_stk1")]
        xk_ld = [sem("xk_ld0"), sem("xk_ld1")]
        c_ld = [sem(f"c_ld{t}") for t in range(TPG)]

        block = ctx.enter_context(nc.Block())

        @block.sync
        def _(sp):
            def load_x(dst, stage, blk):
                b = (stage >> 2) & (NB - 1)
                return sp.dma_start(dst, xT.rearrange("(c p) t -> p c t", p=P)[:, :, bass.ds(b * L + blk * QB, QB)])

            def load_w(dst, which, stage):
                g = stage & (NG - 1)
                return sp.dma_start(dst, wT[which].rearrange("(c p) n -> p c n", p=P)[:, :, bass.ds(g * P, P)])

            def stack(dst, parts, done):
                for r, part in enumerate(parts):
                    sp.dma_start(dst[HD * r:HD * r + HD].bitcast(F32), part.bitcast(F32)).then_inc(done, 16)

            def keys(stage, par):
                for t in range(NQB):
                    wait_alone(sp, vproj, stage * NQB + t + 1, passed)
                    if t < 2:
                        load_x(xk[:, t], stage, t + 2).then_inc(xk_ld[t], 16)
                    else:
                        load_x(xk[:, t - 2], stage + 1, t - 2).then_inc(xk_ld[t - 2], 16)
                    sp.wait_ge(k_hi, stage * NQB + t + 1)
                    sp.wait_ge(k_lo, stage * NQB + t + 1)
                    stack(kst[par][:, :, t * QB:(t + 1) * QB], (hi[:, t % 2], lo[:, t % 2], hi[:, t % 2]),
                          k_stk[t % 2])
                load_w(wkv[:, 0], 1, stage + 1).then_inc(wkv_ld, 16)
                load_w(wkv[:, 1], 2, stage + 1).then_inc(wkv_ld, 16)

            def queries(f):
                sp.wait_ge(qproj, f + 1)
                load_x(xq[:], (f + 1) >> 2, (f + 1) & 3).then_inc(xq_ld, 16)
                sp.wait_ge(q_hi, f + 1)
                sp.wait_ge(q_lo, f + 1)
                stack(qnew[:], (hi[:, 0], hi[:, 0], lo[:, 0]), q_stk)

            def publish(f, j):
                sp.wait_ge(q_stk, (f + 1) * NSTK)
                sp.dma_start(qcur[0:RMASK, bass.ds(j, 1)].rearrange("p a h x -> p (a h x)").bitcast(F32),
                             qnew[0:RMASK].rearrange("p h x -> p (h x)").bitcast(F32)).then_inc(q_cur, 16)
                sp.wait_ge(mcp, f + 1)
                for r in range(2):
                    row = qcur[RM0 + r:RM0 + r + 1, bass.ds(j, 1)].rearrange("p a h x -> p (a h x)")
                    sp.dma_start(row.bitcast(F32), mrow[HG * NQB * r:HG * NQB * (r + 1), :].bitcast(F32)).then_inc(q_cur, 16)
                wait_alone(sp, q_cur, (f + 1) * 48, passed)

            def tokens(b):
                sp.wait_ge(pv, (b + 1) * (NG * NQB * NKC))
                sp.wait_ge(cst, (b + 1) * (NG * NQB * 16))
                sp.dma_start(wo_sb, woT.rearrange("(g p) n -> p g n", p=P)).then_inc(c_par, 16)
                sp.dma_start(gam, gamma.partition_broadcast(P)).then_inc(c_par, 16)
                sp.dma_start(bet, beta.partition_broadcast(P)).then_inc(c_par, 16)
                sp.dma_start(bob, bo.partition_broadcast(P)).then_inc(c_par, 16)
                with sp.Fori(0, NGRP) as gi:
                    grp = b * NGRP + gi
                    for t in range(TPG):
                        tok = gi * (TPG * P) + t * P
                        sp.dma_start(tC[t].rearrange("p (g n) -> p g n", g=NG),
                                     ctxT.rearrange("s p l -> p s l")[:, bass.ds(b * NG, NG), bass.ds(tok, P)])\
                            .then_inc(c_ld[t], 16)
                        sp.dma_start(tA[t], x[bass.ds(b * L + tok, P), :]).then_inc(c_ld[t], 16)
                    for t in range(TPG):
                        sp.wait_ge(c_o, grp * TPG + t + 1)
                        sp.dma_start(out[bass.ds(b * L + gi * (TPG * P) + t * P, P), :], tA[t]).then_inc(c_st, 16)
                    wait_alone(sp, c_st, (grp + 1) * (TPG * 16), passed)

            sp.dma_start(rows[0:1, 8:10, :], band.rearrange("a (b n) -> a b n", b=2)).then_inc(band_ld, 16)
            sp.dma_start(rows[:, 0:4, :], w_ffn.rearrange("(c p) n -> p c n", p=P)).then_inc(wf_ld, 16)
            load_w(wkv[:, 0], 1, 0).then_inc(wkv_ld, 16)
            load_w(wkv[:, 1], 2, 0).then_inc(wkv_ld, 16)
            load_w(wq[:], 0, 0).then_inc(wq_ld, 16)
            sp.dma_start(bias[:], bqkv).then_inc(bias_ld, 16)
            load_x(xk[:, 0], 0, 0).then_inc(xk_ld[0], 16)
            load_x(xk[:, 1], 0, 1).then_inc(xk_ld[1], 16)
            load_x(xq[:], 0, 0).then_inc(xq_ld, 16)
            sp.dma_start(hadm[:], had).then_inc(had_ld, 16)
            sp.wait_ge(stk_ones, 4)
            sp.wait_ge(mask_ok, 2)
            for par in range(2):
                for h in range(HG):
                    sp.dma_start(kst[par][RMASK:RMASK + 1, h].bitcast(F32),
                                 qnew[0:1].rearrange("p h x -> p (h x)").bitcast(F32)).then_inc(mask_ld, 16)
            sp.wait_ge(mask_ld, 2 * HG * 16)
            keys(0, 0)
            with sp.Fori(0, NQB) as j:
                queries(j)
                publish(j, j)
            load_w(wq[:], 0, 1).then_inc(wq_ld, 16)
            with sp.Fori(0, NB) as b:
                with sp.Fori(0, NG // 2) as half:
                    for par in range(2):
                        stage = b * NG + half * 2 + par
                        keys(stage + 1, 1 - par)
                        with sp.Fori(0, NQB) as j:
                            n = stage * NQB + j
                            queries(n + NQB)
                            wait_alone(sp, sc, (n + 1) * (2 * NKC), passed)
                            publish(n + NQB, j)
                        load_w(wq[:], 0, stage + 2).then_inc(wq_ld, 16)
                tokens(b)
            sp.wait_ge(c_st, NS * NQB * 16)
            sp.wait_ge(wkv_ld, (NS + 2) * 32)
            sp.wait_ge(wq_ld, (NS + 2) * 16)
            sp.wait_ge(xq_ld, (NS + 1) * 64 + 16)
            for t in range(2):
                sp.wait_ge(xk_ld[t], (NS + 1) * 32 + 16)

        @block.tensor
        def _(pe):
            def keys(stage, par, first=False):
                pe.wait_ge(wkv_ld, (stage + 1) * 32)
                for t in range(NQB):
                    pe.wait_ge(xk_ld[t % 2], stage * 32 + (t // 2 + 1) * 16)
                    if t > 0:
                        pe.wait_ge(k_lo, stage * NQB + t)
                    elif not first:
                        pe.wait_ge(mcp, stage * NQB)
                    for c in range(IC):
                        mm = nc.tensor.matmul(ps_m[:, 0, :], wkv[:, 0, c], xk[:, t % 2, c], start=c == 0, stop=c == IC - 1)
                    mm.then_inc(kproj, 1)
                    if t > 0:
                        pe.wait_ge(v_cp, stage * NQB + t)
                    for u in range(QB // P):
                        for c in range(IC):
                            mm = nc.tensor.matmul(ps_m[:, 1, u * P:(u + 1) * P], xk[:, t % 2, c, u * P:(u + 1) * P],
                                                  wkv[:, 1, c], start=c == 0, stop=c == IC - 1)
                    mm.then_inc(vproj, 1)

            def queries(f, stage):
                pe.wait_ge(wq_ld, (stage + 1) * 16)
                pe.wait_ge(xq_ld, (f + 1) * 16)
                pe.wait_ge(k_lo, (stage + 1) * NQB)
                for c in range(IC):
                    mm = nc.tensor.matmul(ps_m[:, 0, :], wq[:, c], xq[:, c], start=c == 0, stop=c == IC - 1)
                mm.then_inc(qproj, 1)

            def unit(u, f, stage, par):
                if u == 0:
                    pe.wait_ge(q_stk, (f + 1) * NSTK)
                    for t in range(2):
                        pe.wait_ge(k_stk[t], (stage + 1) * (2 * NSTK))
                    pe.wait_ge(v_cp, (stage + 1) * NQB)
                elif u >= 2:
                    pe.wait_ge(mred, f * UNITS + u - 1)
                m, kb = divmod(u, NQB)
                h, qt = divmod(m, QB // P)
                nc.tensor.matmul(ps_m[:, u % 2, :], qnew[0:RSTACK, h, qt * P:(qt + 1) * P],
                                 kst[par][0:RSTACK, h, kb * QB:(kb + 1) * QB], start=True, stop=True).then_inc(msc, 1)

            def maxima_to_rows(f):
                pe.wait_ge(mneg, f + 1)
                nc.tensor.transpose(ps_m[0:2 * HG * NQB, 0, 0:P], msplit[:], ident[:]).then_inc(mtr, 1)

            def scores(c, p, par, j):
                for h in (2 * p, 2 * p + 1):
                    mm = nc.tensor.matmul(ps_s[:, h, :], kst[par][0:RALL, h, c * P:(c + 1) * P],
                                          qcur[0:RALL, bass.ds(j, 1), h, :].rearrange("p a x -> p (a x)"),
                                          start=True, stop=True)
                mm.then_inc(sc, 1)

            def column_sums(src, first, last):
                for h in range(HG):
                    mm = nc.tensor.matmul(ps_z[HD * h:HD * h + HD, :], ones[:, 0:HD], src[:, h, :], start=first, stop=last)
                return mm

            def attend(n, f, stage, par, j):
                pe.wait_ge(mcp, f)
                queries(f, stage + 1)
                pe.wait_ge(q_cur, (n + 1) * 48)
                scores(0, 0, par, j)
                scores(0, 1, par, j)
                for c in range(NKC):
                    for p in range(2):
                        pe.wait_ge(ex, n * (2 * NKC) + 2 * c + p + 1)
                        if c < NKC - 1:
                            scores(c + 1, p, par, j)
                        for u in units_at.get((c, p), ()):
                            unit(u, f, stage + 1, 1 - par)
                    if c == 0:
                        pe.wait_ge(q_lo, f + 1)
                    for h in range(HG):
                        mm = nc.tensor.matmul(ps_o[HD * h:HD * h + HD, :], vst[:, par, c, HD * h:HD * h + HD],
                                              prob[:, c % 3, h, :], start=c == 0, stop=c == NKC - 1)
                    if c in POOL_CHUNKS:
                        mm.then_inc(pv, 1)
                    for u in units_at.get((c, 2), ()):
                        unit(u, f, stage + 1, 1 - par)
                    if c not in POOL_CHUNKS:
                        column_sums(prob[:, c % 3], c == PE_FIRST, False).then_inc(pv, 1)
                    for u in units_at.get((c, 3), ()):
                        unit(u, f, stage + 1, 1 - par)
                pe.wait_ge(padd, (n + 1) * NADD)
                column_sums(acc, False, True).then_inc(zdone, 1)
                maxima_to_rows(f)

            def tokens(b):
                pe.wait_ge(c_par, (b + 1) * 64)
                pe.wait_ge(cnorm, (b + 1) * (NG * NQB))
                wait_alone(pe, mcp, (b + 1) * (NG * NQB) + NQB, passed)
                with pe.Fori(0, NGRP) as gi:
                    grp = b * NGRP + gi
                    for t in range(TPG):
                        pe.wait_ge(c_ld[t], (grp + 1) * 32)
                        for g in range(NG):
                            mm = nc.tensor.matmul(ps_s[:, t, :], tC[t][:, g * P:(g + 1) * P], wo_sb[:, g, :],
                                                  start=g == 0, stop=g == NG - 1)
                        mm.then_inc(c_wo, 1)
                    for t in range(TPG):
                        pe.wait_ge(c_w, grp * TPG + t + 1)
                        for c in range(IC):
                            mm = nc.tensor.transpose(bank2[t][:, c * P:(c + 1) * P], tC[t][:, c * P:(c + 1) * P], ident[:])
                        mm.then_inc(c_wt, 1)
                    for t in range(TPG):
                        pe.wait_ge(c_wtc, grp * TPG + t + 1)
                        for c in range(IC):
                            mm = nc.tensor.matmul(ps_s[:, t, c * P:(c + 1) * P], tA[t][:, c * P:(c + 1) * P], hadm[:],
                                                  start=True, stop=True)
                        mm.then_inc(c_h, 1)
                    for t in range(TPG):
                        pe.wait_ge(c_q, grp * TPG + t + 1)
                        for c in range(IC):
                            mm = nc.tensor.transpose(bank2[t].bitcast(BF16)[:, c * P:(c + 1) * P],
                                                     tA[t].bitcast(BF16)[:, c * P:(c + 1) * P], identb[:])
                        mm.then_inc(c_qt, 1)
                    for t in range(TPG):
                        pe.wait_ge(c_qtc, grp * TPG + t + 1)
                        for c in range(IC):
                            mm = nc.tensor.matmul(ps_s[:, t, :], tC[t].bitcast(BF16)[:, c * P:(c + 1) * P], ternT[:, c, :],
                                                  start=c == 0, stop=c == IC - 1)
                        mm.then_inc(c_ffn, 1)

            pe.wait_ge(idf, 5)
            pe.wait_ge(tern_ok, 1)
            for c in range(IC):
                for oc in range(IC):
                    nc.tensor.transpose(ps_s[:, c, :].bitcast(BF16)[:, oc * P:(oc + 1) * P],
                                        ternb[:, oc, c * P:(c + 1) * P], identb[:])
            for oc in range(IC):
                mm = nc.tensor.matmul(ps_o[:, oc * P:(oc + 1) * P], ones[:], diag[:, oc * P:(oc + 1) * P], start=True, stop=True)
            mm.then_inc(tern_t, 1)
            pe.wait_ge(mask_ld, 2 * HG * 16)
            pe.wait_ge(tern_c, 5)
            keys(0, 0, first=True)
            with pe.Fori(0, NQB) as j:
                queries(j, 0)
                for u in range(UNITS):
                    unit(u, j, 0, 0)
                maxima_to_rows(j)
                wait_alone(pe, mcp, j + 1, passed)
            with pe.Fori(0, NB) as b:
                with pe.Fori(0, NG // 2) as half:
                    for par in range(2):
                        stage = b * NG + half * 2 + par
                        keys(stage + 1, 1 - par)
                        with pe.Fori(0, NQB) as j:
                            n = stage * NQB + j
                            attend(n, n + NQB, stage, par, j)
                tokens(b)
                wait_alone(pe, c_st, (b + 1) * (NGRP * TPG * 16), passed)

        @block.scalar
        def _(act):
            def bias_of(which, stage):
                return bias[:, bass.ds((stage & (NG - 1)) + which * NG, 1)]

            def keys(stage, par):
                for t in range(NQB):
                    if t >= 2:
                        act.wait_ge(k_stk[t % 2], stage * (2 * NSTK) + NSTK)
                    wait_alone(act, kproj, stage * NQB + t + 1, passed)
                    nc.scalar.activation(hi[:, t % 2], ps_m[:, 0, :], ACT.Identity, bias=bias_of(1, stage)).then_inc(k_hi, 1)
                    act.wait_ge(vproj, stage * NQB + t + 1)
                    nc.scalar.activation(vst[:, par, t * (QB // P):(t + 1) * (QB // P), :].rearrange("p c d -> p (c d)"),
                                         ps_m[:, 1, :], ACT.Copy).then_inc(v_cp, 1)

            def queries(f, stage):
                act.wait_ge(k_stk[0], (stage + 1) * (2 * NSTK))
                wait_alone(act, qproj, f + 1, passed)
                nc.scalar.activation(hi[:, 0], ps_m[:, 0, :], ACT.Identity, bias=bias_of(0, stage)).then_inc(q_hi, 1)

            def maxima_rows(f):
                act.wait_ge(mtr, f + 1)
                nc.scalar.activation(mrow[:], ps_m[0:2 * HG * NQB, 0, 0:P], ACT.Copy).then_inc(mcp, 1)

            def attend(n, f, stage):
                queries(f, stage + 1)
                for c in range(NKC):
                    for p in range(2):
                        act.wait_ge(sc, n * (2 * NKC) + 2 * c + p + 1)
                        if c >= 3 and p == 0:
                            act.wait_ge(pv, n * NKC + c - 2)
                            if c - 3 in POOL_CHUNKS:
                                act.wait_ge(padd, n * NADD + ADD_OF[c - 3] + 1)
                        nc.scalar.activation(prob[:, c % 3, 2 * p:2 * p + 2, :], ps_s[:, 2 * p:2 * p + 2, :],
                                             ACT.Exp, scale=SCALE).then_inc(ex, 1)
                maxima_rows(f)

            def tokens(b):
                with act.Fori(0, NGRP) as gi:
                    grp = b * NGRP + gi
                    for k in range(2):
                        act.wait_ge(c_ve, grp * 3 + k + 1)
                        nc.scalar.activation(lnv[:, :, 1], lnv[:, :, 0], ACT.Sqrt).then_inc(c_sd, 1)
                    for t in range(TPG):
                        act.wait_ge(c_wt, grp * TPG + t + 1)
                        nc.scalar.activation(tA[t], bank2[t], ACT.Copy).then_inc(c_wtc, 1)
                    for t in range(TPG):
                        act.wait_ge(c_q1, grp * TPG + t + 1)
                        act.wait_ge(c_h, grp * TPG + t + 1)
                        nc.scalar.activation(tA[t].bitcast(BF16)[:, 0:D], tC[t], ACT.Copy, bias=-MAGIC).then_inc(c_q, 1)
                    for t in range(TPG):
                        act.wait_ge(c_qt, grp * TPG + t + 1)
                        act.wait_ge(c_q, grp * TPG + t + 1)
                        nc.scalar.activation(tC[t].bitcast(BF16)[:, 0:D], bank2[t].bitcast(BF16)[:, 0:D],
                                             ACT.Copy).then_inc(c_qtc, 1)
                    act.wait_ge(c_ve, grp * 3 + 3)
                    nc.scalar.activation(lnv[:, :, 1], lnv[:, :, 0], ACT.Sqrt).then_inc(c_sd, 1)

            act.wait_ge(band_mx, 1)
            nc.scalar.activation(band_e, band_row, ACT.Exp, bias=band_s[:, 0:1], accum_out=band_s[:, 1:2]).then_inc(band_ex, 1)
            act.wait_ge(bias_ld, 16)
            keys(0, 0)
            with act.Fori(0, NQB) as j:
                queries(j, 0)
                maxima_rows(j)
            with act.Fori(0, NB) as b:
                with act.Fori(0, NG // 2) as half:
                    for par in range(2):
                        stage = b * NG + half * 2 + par
                        keys(stage + 1, 1 - par)
                        with act.Fori(0, NQB) as j:
                            n = stage * NQB + j
                            attend(n, n + NQB, stage)
                tokens(b)
                wait_alone(act, c_st, (b + 1) * (NGRP * TPG * 16), passed)

        @block.vector
        def _(dve):
            def bias_of(which, stage):
                return bias[:, bass.ds((stage & (NG - 1)) + which * NG, 1)]

            def low_part(dst, high, which, stage):
                return nc.vector.scalar_tensor_tensor(out=dst, in0=ps_m[:, 0, :], scalar=bias_of(which, stage),
                                                      in1=high.bitcast(F32), op0=ALU.add, op1=ALU.subtract)

            def keys(stage):
                for t in range(NQB):
                    dve.wait_ge(k_hi, stage * NQB + t + 1)
                    if t >= 2:
                        dve.wait_ge(k_stk[t % 2], stage * (2 * NSTK) + NSTK)
                    low_part(lo[:, t % 2], hi[:, t % 2], 1, stage).then_inc(k_lo, 1)

            def queries(f, stage):
                dve.wait_ge(q_hi, f + 1)
                low_part(lo[:, 0], hi[:, 0], 0, stage).then_inc(q_lo, 1)

            def maxima(f):
                for u in range(UNITS):
                    dve.wait_ge(msc, f * UNITS + u + 1)
                    m, kb = divmod(u, NQB)
                    nc.vector.tensor_reduce(umax[:, m, kb:kb + 1], ps_m[:, u % 2, :], AX.X, ALU.max).then_inc(mred, 1)
                dve.wait_ge(mred, (f + 1) * UNITS)
                nc.vector.tensor_reduce(negm[:], umax[:], AX.X, ALU.max, negate=True).then_inc(mstep, 1)
                dve.wait_ge(mstep, f * 2 + 1)
                nc.vector.tensor_copy(mhi[:], negm[:]).then_inc(mstep, 1)
                dve.wait_ge(mstep, f * 2 + 2)
                nc.vector.tensor_copy(msplit[:, 0:HG * NQB], mhi[:].bitcast(F32))
                nc.vector.tensor_tensor(msplit[:, HG * NQB:], negm[:], mhi[:].bitcast(F32), ALU.subtract).then_inc(mneg, 1)

            def normalise(n, stage):
                dve.wait_ge(zdone, n + 1)
                nc.vector.reciprocal(acc[:, 0, :], ps_z[:]).then_inc(zinv, 1)
                dve.wait_ge(zinv, n + 1)
                nc.vector.tensor_tensor(acc[:, 1, :], ps_o[:], acc[:, 0, :], ALU.mult).then_inc(cnorm, 1)
                dve.wait_ge(cnorm, n + 1)
                nc.vector.tensor_scalar(acc[:, 2, :], acc[:, 1, :], bias_of(2, stage), None, ALU.add).then_inc(cbias, 1)

            def tokens(b):
                wait_alone(dve, c_par, (b + 1) * 64, passed)
                with dve.Fori(0, NGRP) as gi:
                    grp = b * NGRP + gi
                    steps = [0]

                    def mark(ins):
                        steps[0] += 1
                        ins.then_inc(c_dve, 1)
                        return steps[0]

                    def own(k):
                        dve.wait_ge(c_dve, grp * C_DVE + k)

                    def statistics(t, src):
                        k = mark(nc.vector.bn_stats(stats[:, t, :], src))
                        wait_alone(dve, c_dve, grp * C_DVE + k, passed)
                        return mark(nc.vector.bn_aggr(mv[:, t, :], stats[:, t, :]))

                    def variances(last):
                        own(last)
                        nc.vector.tensor_scalar(lnv[:, :, 0], mv[:, :, 1], LN_EPS, None, ALU.add).then_inc(c_ve, 1)

                    def inverse_roots(k):
                        dve.wait_ge(c_sd, grp * 3 + k)
                        v, s, r, w = (lnv[:, :, i] for i in range(4))
                        own(mark(nc.vector.reciprocal(r, s)))
                        own(mark(nc.vector.tensor_tensor(w, r, r, ALU.mult)))
                        own(mark(nc.vector.tensor_tensor(w, w, v, ALU.mult)))
                        own(mark(nc.vector.tensor_scalar(w, w, -0.5, 1.5, ALU.mult, ALU.add)))
                        own(mark(nc.vector.tensor_tensor(r, r, w, ALU.mult)))

                    def normal(t, buf):
                        return nc.vector.tensor_scalar(buf, buf, mv[:, t, 0:1], lnv[:, t, 2:3], ALU.subtract, ALU.mult)

                    for t in range(TPG):
                        dve.wait_ge(c_wo, grp * TPG + t + 1)
                        dve.wait_ge(c_xb, grp * TPG + t + 1)
                        own(mark(nc.vector.tensor_tensor(tB[t], ps_s[:, t, :], tB[t], ALU.add)))
                        last = statistics(t, tB[t])
                    variances(last)
                    inverse_roots(1)
                    for t in range(TPG):
                        normal(t, tB[t]).then_inc(c_n1, 1)
                    for t in range(TPG):
                        dve.wait_ge(c_ng, grp * TPG + t + 1)
                        own(mark(nc.vector.tensor_tensor(tB[t], tB[t], tA[t], ALU.add)))
                        last = statistics(t, tB[t])
                    variances(last)
                    inverse_roots(2)
                    for t in range(TPG):
                        normal(t, tB[t]).then_inc(c_x1, 1)
                    for t in range(TPG):
                        dve.wait_ge(c_h, grp * TPG + t + 1)
                        last = mark(nc.vector.tensor_reduce(qsc[:, t, 0:1], ps_s[:, t, :], AX.X, ALU.max,
                                                            apply_absolute_value=True))
                    own(last)
                    own(mark(nc.vector.tensor_scalar(qsc[:, :, 1], qsc[:, :, 0], 1e-5, 1.0 / 7.0, ALU.max, ALU.mult)))
                    own(mark(nc.vector.reciprocal(qsc[:, :, 2], qsc[:, :, 1])))
                    for t in range(TPG):
                        own(mark(nc.vector.tensor_scalar(tC[t], ps_s[:, t, :], qsc[:, t, 2:3], 7.0, ALU.mult, ALU.min)))
                        nc.vector.tensor_scalar(tC[t], tC[t], -8.0, MAGIC, ALU.max, ALU.add).then_inc(c_q1, 1)
                    for t in range(TPG):
                        dve.wait_ge(c_ffn, grp * TPG + t + 1)
                        own(mark(nc.vector.scalar_tensor_tensor(out=tA[t], in0=ps_s[:, t, :], scalar=qsc[:, t, 1:2],
                                                                in1=wscale[:], op0=ALU.mult, op1=ALU.mult)))
                        own(mark(nc.vector.tensor_tensor(tA[t], tA[t], tB[t], ALU.add)))
                        last = statistics(t, tA[t])
                    variances(last)
                    inverse_roots(3)
                    for t in range(TPG):
                        normal(t, tA[t]).then_inc(c_o, 1)
                    assert steps[0] == C_DVE, steps[0]

            done = [0]

            def step(ins):
                done[0] += 1
                ins.then_inc(dstep, 1)
                dve.wait_ge(dstep, done[0])

            dve.wait_ge(band_ld, 16)
            nc.vector.tensor_reduce(band_s[:, 0:1], band_row, AX.X, ALU.max, negate=True).then_inc(band_mx, 1)
            step(nc.vector.memset(band_e_pad, PAD))
            dve.wait_ge(band_ex, 1)
            step(nc.vector.reciprocal(band_s[:, 2:3], band_s[:, 1:2]))
            step(nc.vector.tensor_scalar(band_e, band_e, band_s[:, 2:3], None, ALU.mult))
            step(nc.vector.max(band_s[:, 8:16], band_all))
            step(nc.vector.memset(band_s[:, 8 + TOPK:16], PAD))
            step(nc.vector.match_replace(out=band_all2, in_to_replace=band_s[:, 8:16], in_values=band_all, imm_value=FOUND))
            nc.vector.tensor_scalar(qmask[:, 0:LBAND], band_all2[:, 0:LBAND], FOUND, MASKED, ALU.is_equal, ALU.mult)\
                .then_inc(mask_ok, 1)
            dve.wait_ge(wf_ld, 16)
            step(nc.vector.tensor_reduce(small[:, 0:IC], wf, AX.X, ALU.add, apply_absolute_value=True))
            step(nc.vector.tensor_scalar(small[:, 0:IC], small[:, 0:IC], 1.0 / D, 1e-5, ALU.mult, ALU.max))
            step(nc.vector.tensor_scalar(small[:, 4:4 + IC], small[:, 0:IC], 0.5, None, ALU.mult))
            step(nc.vector.tensor_scalar(small[:, 8:8 + IC], small[:, 0:IC], -0.5, None, ALU.mult))
            dve.wait_ge(idf, 5)
            for oc in range(IC):
                step(nc.vector.tensor_scalar(neg, wf[:, oc], small[:, 8 + oc:9 + oc], None, ALU.is_lt))
                step(nc.vector.scalar_tensor_tensor(out=ternb[:, oc], in0=wf[:, oc], scalar=small[:, 4 + oc:5 + oc], in1=neg,
                                                    op0=ALU.is_gt, op1=ALU.subtract))
                ins = nc.vector.tensor_scalar(diag[:, oc * P:(oc + 1) * P], ident[:], small[:, oc:oc + 1], None, ALU.mult)
                if oc < IC - 1:
                    step(ins)
            ins.then_inc(tern_ok, 1)
            dve.wait_ge(tern_t, 1)
            for c in range(IC):
                nc.vector.tensor_copy(ternT[:, c, :], ps_s[:, c, :].bitcast(BF16)[:, 0:D]).then_inc(tern_c, 1)
            nc.vector.tensor_copy(wscale[:], ps_o[:]).then_inc(tern_c, 1)
            dve.wait_ge(bias_ld, 16)
            keys(0)
            with dve.Fori(0, NQB) as j:
                queries(j, 0)
                maxima(j)
            with dve.Fori(0, NB) as b:
                with dve.Fori(0, NG // 2) as half:
                    for par in range(2):
                        stage = b * NG + half * 2 + par
                        keys(stage + 1)
                        with dve.Fori(0, NQB) as j:
                            n = stage * NQB + j
                            queries(n + NQB, stage + 1)
                            maxima(n + NQB)
                            normalise(n, stage)
                tokens(b)
                wait_alone(dve, c_st, (b + 1) * (NGRP * TPG * 16), passed)

        @block.gpsimd
        def _(pool):
            def attend(n, stage, j):
                for i in range(NADD):
                    c = POOL_CHUNKS[i + 1]
                    pool.wait_ge(ex, n * (2 * NKC) + 2 * c + 2)
                    if i == 0:
                        a = prob[:, POOL_CHUNKS[0] % 3]
                    else:
                        pool.wait_ge(padd, n * NADD + i)
                        a = acc[:]
                    nc.gpsimd.tensor_tensor(acc[:], a, prob[:, c % 3], ALU.add).then_inc(padd, 1)
                pool.wait_ge(cbias, n + 1)
                nc.gpsimd.dma_start(ctxT[bass.ds(stage, 1), :, bass.ds(j * QB, QB)].rearrange("s p l -> p (s l)"),
                                    acc[:, 2, :]).then_inc(cst, 16)
                wait_alone(pool, cst, (n + 1) * 16, passed)

            def tokens(b):
                wait_alone(pool, c_par, (b + 1) * 64, passed)
                with pool.Fori(0, NGRP) as gi:
                    grp = b * NGRP + gi
                    for t in range(TPG):
                        pool.wait_ge(c_ld[t], (grp + 1) * 32)
                        nc.gpsimd.tensor_tensor(tB[t], tA[t], bob, ALU.add).then_inc(c_xb, 1)
                    for t in range(TPG):
                        pool.wait_ge(c_xb, grp * TPG + t + 1)
                        nc.gpsimd.tensor_tensor(tA[t], tA[t], bet, ALU.add).then_inc(c_xg, 1)
                    for t in range(TPG):
                        pool.wait_ge(c_n1, grp * TPG + t + 1)
                        pool.wait_ge(c_xg, grp * TPG + t + 1)
                        nc.gpsimd.tensor_tensor(tB[t], tB[t], gam, ALU.mult).then_inc(c_ng, 1)
                    for t in range(TPG):
                        pool.wait_ge(c_x1, grp * TPG + t + 1)
                        a, s, o = tB[t], tA[t], tC[t]
                        half = D // 2
                        nc.gpsimd.tensor_tensor(s[:, 0:half], a[:, 0:half], a[:, half:], ALU.add).then_inc(c_ws, 1)
                        nc.gpsimd.tensor_tensor(s[:, half:], a[:, 0:half], a[:, half:], ALU.subtract).then_inc(c_ws, 1)
                        pool.wait_ge(c_ws, (grp * TPG + t + 1) * 3 - 1)
                        sv = s.rearrange("p (a b n) -> p a b n", a=2, b=2)
                        ov = o.rearrange("p (a b n) -> p a b n", a=2, b=2)
                        nc.gpsimd.tensor_tensor(ov[:, :, 0, :], sv[:, :, 0, :], sv[:, :, 1, :], ALU.add).then_inc(c_ws, 1)
                        nc.gpsimd.tensor_tensor(ov[:, :, 1, :], sv[:, :, 0, :], sv[:, :, 1, :], ALU.subtract)\
                            .then_inc(c_w, 1)

            nc.gpsimd.memset(ones[:], 1.0).then_inc(idf, 1)
            pool.wait_ge(idf, 1)
            nc.gpsimd.memset(ident[:], 0.0).then_inc(idf, 1)
            pool.wait_ge(idf, 2)
            nc.gpsimd.affine_select(out=ident[:], in_=ident[:], compare_op=ALU.not_equal, fill=1.0, base=0,
                                    pattern=[[-1, P]], channel_multiplier=1).then_inc(idf, 2)
            pool.wait_ge(idf, 4)
            nc.gpsimd.tensor_copy(identb[:], ident[:]).then_inc(idf, 1)
            pool.wait_ge(idf, 5)
            nc.gpsimd.memset(qmask[:, LBAND:].bitcast(F32), 0.0).then_inc(mask_ok, 1)
            nc.gpsimd.memset(qcur[RMASK:RALL].bitcast(F32), 1.0).then_inc(stk_ones, 1)
            pool.wait_ge(stk_ones, 1)
            nc.gpsimd.memset(qnew[RMASK:RSTACK].bitcast(F32), 1.0).then_inc(stk_ones, 1)
            for i in range(2):
                pool.wait_ge(stk_ones, 2 + i)
                nc.gpsimd.memset(kst[i][RMASK:RALL].bitcast(F32), 1.0).then_inc(stk_ones, 1)
            pool.wait_ge(stk_ones, 4)
            pool.wait_ge(mask_ok, 2)
            with pool.Fori(0, NB) as b:
                with pool.Fori(0, NG) as g:
                    stage = b * NG + g
                    with pool.Fori(0, NQB) as j:
                        attend(stage * NQB + j, stage, j)
                tokens(b)
                wait_alone(pool, c_st, (b + 1) * (NGRP * TPG * 16), passed)


def kernel(L0_attn_x, L0_attn_band_importance, L0_attn_Wq, L0_attn_bq, L0_attn_Wk, L0_attn_bk, L0_attn_Wv, L0_attn_bv,
           L0_attn_Wo, L0_attn_bo, L0_attn_gamma, L0_attn_beta, L0_ffn_weight):
    import concourse.bacc as bacc
    from concourse.bass_utils import run_bass_kernel_spmd

    nc = bacc.Bacc("TRN2", target_bir_lowering=False, num_devices=1)
    x = np.asarray(L0_attn_x).reshape(NB * L, D)
    h = np.ones((1, 1), np.float32)
    while h.shape[0] < P:
        h = np.block([[h, h], [h, -h]])

    def interleave(a):
        return a.reshape(-1, NG, HG, HD).transpose(0, 1, 3, 2).reshape(a.shape)

    wq, wk, wv = (np.asarray(w).T for w in (L0_attn_Wq, L0_attn_Wk, L0_attn_Wv))
    bq, bk, bv = (np.asarray(v) for v in (L0_attn_bq, L0_attn_bk, L0_attn_bv))
    arrays = {
        "x": x,
        "xT": x.T,
        "wT": np.stack([interleave(wq), interleave(wk), wv]),
        "bqkv": np.stack([v.reshape(NG, P).T for v in (interleave(bq), interleave(bk), bv)], 1).reshape(P, 3 * NG),
        "woT": np.asarray(L0_attn_Wo).T,
        "w_ffn": L0_ffn_weight,
        "band": L0_attn_band_importance,
        "gamma": L0_attn_gamma,
        "beta": L0_attn_beta,
        "bo": L0_attn_bo,
        "had": (h / np.sqrt(D)).astype(np.float32),
    }
    arrays = {f"in_{k}_dram": np.ascontiguousarray(v) for k, v in arrays.items()}
    args = [nc.dram_tensor(k, v.shape, mybir.dt.from_np(v.dtype), kind="ExternalInput").ap() for k, v in arrays.items()]
    out = nc.dram_tensor("out_dram", (NB * L, D), F32, kind="ExternalOutput").ap()
    build(nc, *args, out)
    r = run_bass_kernel_spmd(nc, [arrays], core_ids=[0])
    return r.results[0]["out_dram"].reshape(NB, L, D)
```

```python
from contextlib import ExitStack

import numpy as np

import concourse.bass as bass
from concourse import mybir

ALU = mybir.AluOpType
ACT = mybir.ActivationFunctionType
AX = mybir.AxisListType
F32 = mybir.dt.float32
F32R = mybir.dt.float32r
BF16 = mybir.dt.bfloat16

P = 128
NB, L, D = 4, 2048, 512
NH, HD = 16, 32
LBAND = 1024
TOPK = 3
HG = 4
NG = NH // HG
NS = NB * NG
IC = D // P
QB = 512
NQB = L // QB
NKC = L // P
UNITS = HG * (QB // P) * NQB
SCALE = 1.0 / float(np.sqrt(HD))
LN_EPS = 1e-5
MASKED = -2.0 ** 80
MAGIC = 1.5 * 2.0 ** 23
RMASK, RM0, RSTACK, RALL = 96, 97, 97, 99
PAD, FOUND = -5.0, -7.0
NPB = 4
NSTK = 3 * 16

POOL_CHUNKS = [0, 1, 2, 4, 5, 7, 8, 10, 11]
NADD = len(POOL_CHUNKS) - 1
ADD_OF = {c: max(i - 1, 0) for i, c in enumerate(POOL_CHUNKS)}
PE_FIRST = next(c for c in range(NKC) if c not in POOL_CHUNKS)
FIRST_UNITS = 1
TPG = 2
NPAIR = L // P // TPG
CHAINS = 2 * NPAIR + 1
D_FIRST, D_BOTH, D_LAST = 28, 42, 19
D_BATCH = D_FIRST + (NPAIR - 1) * D_BOTH + D_LAST


def unit_steps():
    places = [(c, i) for c in range(FIRST_UNITS, NKC - 1) for i in ((0, 1, 2, 2) if c in POOL_CHUNKS else (0, 1, 1, 2, 2, 3))]
    steps = {}
    for u in range(UNITS):
        steps.setdefault(places[u * len(places) // UNITS], []).append(u)
    return steps


def wait_alone(eng, sem, value, passed):
    eng.wait_ge(sem, value)
    eng.sem_inc(passed, 1)


def pair_steps(eng, step):
    step(0, 0, True, False)
    step(1, 1, True, True)
    with eng.Fori(0, (NPAIR - 2) // 2) as i:
        for par in range(2):
            step(i * 2 + (2 + par), par, True, True)
    step(NPAIR, 0, False, True)


def build(nc, x, xT, wT, bqkv, woT, w_ffn, band, gamma, beta, bo, had, out):
    units_at = unit_steps()
    ctxT = nc.dram_tensor("ctxT_dram", (NS, P, L), F32, kind="Internal").ap()

    with ExitStack() as ctx:
        def sb(name, shape, dt=F32):
            return ctx.enter_context(nc.sbuf_tensor(name, shape, dt))

        def sem(name):
            return ctx.enter_context(nc.semaphore(name))

        kst = [sb(f"kst{i}", [P, HG, L], F32R) for i in range(2)]
        qcur = sb("qcur", [P, NQB, HG, QB], F32R)
        qnew = sb("qnew", [P, HG, QB], F32R)
        vst = sb("vst", [P, 2, NKC, P])
        prob = sb("prob", [P, NPB, HG, QB])
        acc = sb("acc", [P, HG, QB])
        xk = sb("xk", [P, 2, IC, QB])
        xq = sb("xq", [P, IC, QB])
        wkv = sb("wkv", [P, 2, IC, P])
        wq = sb("wq", [P, IC, P])
        bias = sb("bias", [P, 3 * NG])
        hi = sb("hi", [P, 2, QB], F32R)
        lo = sb("lo", [P, 2, QB], F32R)
        umax = sb("umax", [P, UNITS // NQB, NQB])
        negm = sb("negm", [P, HG * NQB])
        msplit = sb("msplit", [P, 2 * HG * NQB])
        mhi = sb("mhi", [P, HG * NQB], F32R)
        mrow = sb("mrow", [2 * HG * NQB, P], F32R)
        ident = sb("ident", [P, P])
        identb = sb("identb", [P, P], BF16)
        ones = sb("ones", [P, P])
        hadm = sb("hadm", [P, P])
        ternT = sb("ternT", [P, IC, D], BF16)
        wscale = sb("wscale", [P, D])
        small = sb("small", [P, 64])
        band_buf = vst[0:1].rearrange("p a c d -> p (a c d)")[:, 0:2 * (LBAND + 8)].rearrange("p (a n) -> p a n", a=2)
        stats = sb("stats", [P, 2 * TPG, 6])
        mv = sb("mv", [P, 2 * TPG, 2])
        lnv = sb("lnv", [P, 2 * TPG, 4])
        qsc = sb("qsc", [P, TPG, 4])

        rows = prob[:].rearrange("p a b c -> p (a b) c")
        tS = [rows[:, t, :] for t in range(2)]
        tA = [[rows[:, 2 + 10 * i + t, :] for t in range(2)] for i in range(2)]
        tW = [[rows[:, 4 + 2 * i + t, :] for t in range(2)] for i in range(2)]
        tR = [[rows[:, 8 + 2 * i + t, :] for t in range(2)] for i in range(2)]
        tC = [hi[:, t, :].bitcast(F32) for t in range(2)]
        tX = [lo[:, t, :].bitcast(F32) for t in range(2)]
        wo_sb = vst[:, 1].rearrange("p c d -> p (c d)").rearrange("p (g n) -> p g n", g=IC)
        gam, bet, bob = acc[:, 0, :], acc[:, 1, :], acc[:, 2, :]

        ps_s = ctx.enter_context(nc.psum_tensor("ps_s", [P, HG, QB], F32))
        ps_o = ctx.enter_context(nc.psum_tensor("ps_o", [P, QB], F32))
        ps_z = ctx.enter_context(nc.psum_tensor("ps_z", [P, QB], F32))
        ps_m = ctx.enter_context(nc.psum_tensor("ps_m", [P, 2, QB], F32))
        ps_wo = [ps_s[:, t, :] for t in range(2)]
        ps_h = [ps_s[:, 2 + t, :] for t in range(2)]
        ps_t = [ps_o[:, :], ps_z[:, :]]


        zbuf, obuf = (prob[:, (NKC - 1) % NPB, h, :] for h in (2, 3))

        wf = rows[:, 0:4, :]
        ternb = rows[:, 4:6, :].rearrange("p a n -> p (a n)").bitcast(BF16).rearrange("p (c n) -> p c n", c=IC)
        neg, diag = rows[:, 6, :], rows[:, 7, :]
        band_row = rows[0:1, 8:10, :].rearrange("p a n -> p (a n)")
        band_all = band_buf[0:1, 0, :]
        band_e, band_e_pad = band_all[:, 0:LBAND], band_all[:, LBAND:]
        band_all2 = band_buf[0:1, 1, :]
        band_s = small[0:1, 16:32]
        qmask = qnew[0:1].rearrange("p h x -> p (h x)")

        passed = sem("passed")
        band_ld = sem("band_ld")
        wf_ld = sem("wf_ld")
        had_ld = sem("had_ld")
        bias_ld = sem("bias_ld")
        mask_ld = sem("mask_ld")
        wkv_ld = sem("wkv_ld")
        wq_ld = sem("wq_ld")
        xq_ld = sem("xq_ld")
        q_stk = sem("q_stk")
        q_copy = sem("q_copy")
        q_cur = sem("q_cur")
        cst = sem("cst")
        c_par = sem("c_par")
        c_st = sem("c_st")
        stk_ones = sem("stk_ones")
        idf = sem("idf")
        mask_ok = sem("mask_ok")
        band_mx = sem("band_mx")
        band_ex = sem("band_ex")
        dstep = sem("dstep")
        tern_ok = sem("tern_ok")
        tern_t = sem("tern_t")
        tern_c = sem("tern_c")
        kproj = sem("kproj")
        vproj = sem("vproj")
        qproj = sem("qproj")
        k_hi = sem("k_hi")
        k_lo = sem("k_lo")
        v_cp = sem("v_cp")
        q_hi = sem("q_hi")
        q_lo = sem("q_lo")
        msc = sem("msc")
        mred = sem("mred")
        mstep = sem("mstep")
        mneg = sem("mneg")
        mtr = sem("mtr")
        mcp = sem("mcp")
        sc = sem("sc")
        ex = sem("ex")
        pv = sem("pv")
        padd = sem("padd")
        zdone = sem("zdone")
        zinv = sem("zinv")
        oz_cp = sem("oz_cp")
        cnorm = sem("cnorm")
        cbias = sem("cbias")
        c_xb = sem("c_xb")
        c_xg = sem("c_xg")
        c_wo = sem("c_wo")
        c_ve = sem("c_ve")
        c_sd = sem("c_sd")
        c_n1 = sem("c_n1")
        c_ng = sem("c_ng")
        c_x1 = sem("c_x1")
        c_w = sem("c_w")
        c_wt = sem("c_wt")
        c_wtc = sem("c_wtc")
        c_h = sem("c_h")
        c_q1 = sem("c_q1")
        c_q = sem("c_q")
        c_qt = sem("c_qt")
        c_qtc = sem("c_qtc")
        c_ffn = sem("c_ffn")
        c_o = sem("c_o")
        c_dve = sem("c_dve")
        k_stk = [sem("k_stk0"), sem("k_stk1")]
        xk_ld = [sem("xk_ld0"), sem("xk_ld1")]
        c_ldc = [sem(f"c_ldc{t}") for t in range(TPG)]
        c_ldx = [sem(f"c_ldx{t}") for t in range(TPG)]

        block = ctx.enter_context(nc.Block())

        @block.sync
        def _(sp):
            def load_x(dst, stage, blk):
                b = (stage >> 2) & (NB - 1)
                return sp.dma_start(dst, xT.rearrange("(c p) t -> p c t", p=P)[:, :, bass.ds(b * L + blk * QB, QB)])

            def load_w(dst, which, stage):
                g = stage & (NG - 1)
                return sp.dma_start(dst, wT[which].rearrange("(c p) n -> p c n", p=P)[:, :, bass.ds(g * P, P)])

            def stack(dst, parts, done):
                for r, part in enumerate(parts):
                    sp.dma_start(dst[HD * r:HD * r + HD].bitcast(F32), part.bitcast(F32)).then_inc(done, 16)

            def keys(stage, par):
                for t in range(NQB):
                    wait_alone(sp, vproj, stage * NQB + t + 1, passed)
                    if t < 2:
                        load_x(xk[:, t], stage, t + 2).then_inc(xk_ld[t], 16)
                    else:
                        load_x(xk[:, t - 2], stage + 1, t - 2).then_inc(xk_ld[t - 2], 16)
                    sp.wait_ge(k_hi, stage * NQB + t + 1)
                    sp.wait_ge(k_lo, stage * NQB + t + 1)
                    stack(kst[par][:, :, t * QB:(t + 1) * QB], (hi[:, t % 2], lo[:, t % 2], hi[:, t % 2]),
                          k_stk[t % 2])
                load_w(wkv[:, 0], 1, stage + 1).then_inc(wkv_ld, 16)
                load_w(wkv[:, 1], 2, stage + 1).then_inc(wkv_ld, 16)

            def queries(f):
                sp.wait_ge(q_hi, f + 1)
                sp.wait_ge(q_lo, f + 1)
                stack(qnew[:], (hi[:, 0], hi[:, 0], lo[:, 0]), q_stk)
                load_x(xq[:], (f + 1) >> 2, (f + 1) & 3).then_inc(xq_ld, 16)
                load_w(wq[:], 0, (f + 1) >> 2).then_inc(wq_ld, 16)

            def copy(f, j):
                sp.wait_ge(q_stk, (f + 1) * NSTK)
                sp.dma_start(qcur[0:RMASK, bass.ds(j, 1)].rearrange("p a h x -> p (a h x)").bitcast(F32),
                             qnew[0:RMASK].rearrange("p h x -> p (h x)").bitcast(F32)).then_inc(q_copy, 16)
                wait_alone(sp, q_copy, (f + 1) * 16, passed)

            def maxima(f, j):
                sp.wait_ge(mcp, f + 1)
                for r in range(2):
                    row = qcur[RM0 + r:RM0 + r + 1, bass.ds(j, 1)].rearrange("p a h x -> p (a h x)")
                    sp.dma_start(row.bitcast(F32), mrow[HG * NQB * r:HG * NQB * (r + 1), :].bitcast(F32)).then_inc(q_cur, 16)

            def store_context(n, stage, j):
                wait_alone(sp, cbias, n + 1, passed)
                sp.dma_start(ctxT[bass.ds(stage, 1), :, bass.ds(j * QB, QB)].rearrange("s p l -> p (s l)"), obuf)\
                    .then_inc(cst, 16)

            def tokens(b):
                wait_alone(sp, pv, (b + 1) * (NG * NQB * NKC), passed)
                sp.wait_ge(cst, (b + 1) * (NG * NQB * 16) + 16)
                sp.dma_start(wo_sb, woT.rearrange("(g p) n -> p g n", p=P)).then_inc(c_par, 16)
                sp.dma_start(gam, gamma.partition_broadcast(P)).then_inc(c_par, 16)
                sp.dma_start(bet, beta.partition_broadcast(P)).then_inc(c_par, 16)
                sp.dma_start(bob, bo.partition_broadcast(P)).then_inc(c_par, 16)
                for t in range(2):
                    sp.wait_ge(k_stk[t], (b * NG + NG + 1) * (2 * NSTK))
                sp.wait_ge(q_stk, (b * (NG * NQB) + NG * NQB + NQB + 1) * NSTK)

                def load_context(k, t):
                    sp.dma_start(tC[t].rearrange("p (g n) -> p g n", g=NG),
                                 ctxT.rearrange("s p l -> p s l")[:, bass.ds(b * NG, NG), bass.ds(k * (TPG * P) + t * P, P)])\
                        .then_inc(c_ldc[t], 16)

                def load_rows(k, t):
                    sp.dma_start(tX[t], x[bass.ds(b * L + k * (TPG * P) + t * P, P), :]).then_inc(c_ldx[t], 16)

                def load_next(k):
                    g = b * NPAIR + k
                    for t in range(TPG):
                        sp.wait_ge(c_wo, g * TPG + t + 1)
                        load_context(k + 1, t)
                    for t in range(TPG):
                        sp.wait_ge(c_xg, g * TPG + t + 1)
                        load_rows(k + 1, t)

                def store(k, par, former=True):
                    if former:
                        sp.wait_ge(c_st, (b * NPAIR + k) * (TPG * 16))
                    for t in range(TPG):
                        sp.wait_ge(c_o, (b * NPAIR + k) * TPG + t + 1)
                        sp.dma_start(out[bass.ds(b * L + k * (TPG * P) + t * P, P), :], tA[par][t]).then_inc(c_st, 16)

                for t in range(TPG):
                    load_context(0, t)
                    load_rows(0, t)
                load_next(0)
                load_next(1)
                store(0, 0, former=False)
                with sp.Fori(0, (NPAIR - 4) // 2) as i:
                    for par in range(2):
                        load_next(i * 2 + (2 + par))
                        store(i * 2 + (1 + par), 1 - par)
                load_next(NPAIR - 2)
                store(NPAIR - 3, 1)
                store(NPAIR - 2, 0)
                store(NPAIR - 1, 1)
                wait_alone(sp, c_st, (b + 1) * (NPAIR * TPG * 16), passed)

            sp.dma_start(rows[0:1, 8:10, :], band.rearrange("a (b n) -> a b n", b=2)).then_inc(band_ld, 16)
            sp.dma_start(rows[:, 0:4, :], w_ffn.rearrange("(c p) n -> p c n", p=P)).then_inc(wf_ld, 16)
            load_w(wkv[:, 0], 1, 0).then_inc(wkv_ld, 16)
            load_w(wkv[:, 1], 2, 0).then_inc(wkv_ld, 16)
            load_w(wq[:], 0, 0).then_inc(wq_ld, 16)
            sp.dma_start(bias[:], bqkv).then_inc(bias_ld, 16)
            load_x(xk[:, 0], 0, 0).then_inc(xk_ld[0], 16)
            load_x(xk[:, 1], 0, 1).then_inc(xk_ld[1], 16)
            load_x(xq[:], 0, 0).then_inc(xq_ld, 16)
            sp.dma_start(hadm[:], had).then_inc(had_ld, 16)
            sp.sem_inc(cst, 16)
            sp.wait_ge(stk_ones, 4)
            sp.wait_ge(mask_ok, 2)
            for par in range(2):
                for h in range(HG):
                    sp.dma_start(kst[par][RMASK:RMASK + 1, h].bitcast(F32),
                                 qnew[0:1].rearrange("p h x -> p (h x)").bitcast(F32)).then_inc(mask_ld, 16)
            sp.wait_ge(mask_ld, 2 * HG * 16)
            keys(0, 0)
            queries(0)
            with sp.Fori(0, NQB) as j:
                copy(j, j)
                queries(j + 1)
                maxima(j, j)
            with sp.Fori(0, NB) as b:
                with sp.Fori(0, NG // 2) as half:
                    for par in range(2):
                        stage = b * NG + half * 2 + par
                        keys(stage + 1, 1 - par)
                        with sp.Fori(0, NQB) as j:
                            n = stage * NQB + j
                            wait_alone(sp, sc, (n + 1) * (2 * NKC), passed)
                            copy(n + NQB, j)
                            queries(n + (NQB + 1))
                            maxima(n + NQB, j)
                            store_context(n, stage, j)
                tokens(b)
            sp.wait_ge(c_st, NS * NQB * 16)
            sp.wait_ge(wkv_ld, (NS + 2) * 32)
            sp.wait_ge(wq_ld, ((NS + 1) * NQB + 2) * 16)
            sp.wait_ge(xq_ld, ((NS + 1) * NQB + 2) * 16)
            sp.wait_ge(q_cur, (NS + 1) * NQB * 32)
            for t in range(2):
                sp.wait_ge(xk_ld[t], (NS + 1) * 32 + 16)

        @block.tensor
        def _(pe):
            def keys(stage, par, first=False):
                pe.wait_ge(wkv_ld, (stage + 1) * 32)
                for t in range(NQB):
                    pe.wait_ge(xk_ld[t % 2], stage * 32 + (t // 2 + 1) * 16)
                    if t > 0:
                        pe.wait_ge(k_lo, stage * NQB + t)
                    elif not first:
                        pe.wait_ge(q_lo, stage * NQB + 1)
                    for c in range(IC):
                        mm = nc.tensor.matmul(ps_m[:, 0, :], wkv[:, 0, c], xk[:, t % 2, c], start=c == 0, stop=c == IC - 1)
                    mm.then_inc(kproj, 1)
                    if t > 0:
                        pe.wait_ge(v_cp, stage * NQB + t)
                    elif not first:
                        pe.wait_ge(mcp, stage * NQB)
                    for u in range(QB // P):
                        for c in range(IC):
                            mm = nc.tensor.matmul(ps_m[:, 1, u * P:(u + 1) * P], xk[:, t % 2, c, u * P:(u + 1) * P],
                                                  wkv[:, 1, c], start=c == 0, stop=c == IC - 1)
                    mm.then_inc(vproj, 1)

            def queries(f, first=False):
                pe.wait_ge(wq_ld, (f + 1) * 16)
                pe.wait_ge(xq_ld, (f + 1) * 16)
                if first:
                    pe.wait_ge(k_lo, NQB)
                else:
                    pe.wait_ge(mred, f * UNITS)
                for c in range(IC):
                    mm = nc.tensor.matmul(ps_m[:, 0, :], wq[:, c], xq[:, c], start=c == 0, stop=c == IC - 1)
                mm.then_inc(qproj, 1)

            def unit(u, f, stage, par, first=False):
                if u == 0:
                    pe.wait_ge(q_stk, (f + 1) * NSTK)
                    for t in range(2):
                        pe.wait_ge(k_stk[t], (stage + 1) * (2 * NSTK))
                    pe.wait_ge(v_cp, (stage + 1) * NQB)
                elif u == 1 and not first:
                    pe.wait_ge(mcp, f)
                elif u >= 2:
                    pe.wait_ge(mred, f * UNITS + u - 1)
                m, kb = divmod(u, NQB)
                h, qt = divmod(m, QB // P)
                nc.tensor.matmul(ps_m[:, u % 2, :], qnew[0:RSTACK, h, qt * P:(qt + 1) * P],
                                 kst[par][0:RSTACK, h, kb * QB:(kb + 1) * QB], start=True, stop=True).then_inc(msc, 1)

            def maxima_to_rows(f, first=False):
                if not first:
                    pe.wait_ge(q_cur, f * 32)
                pe.wait_ge(mneg, f + 1)
                nc.tensor.transpose(ps_m[0:2 * HG * NQB, 1, 0:P], msplit[:], ident[:]).then_inc(mtr, 1)

            def scores(c, p, par, j):
                for h in (2 * p, 2 * p + 1):
                    mm = nc.tensor.matmul(ps_s[:, h, :], kst[par][0:RALL, h, c * P:(c + 1) * P],
                                          qcur[0:RALL, bass.ds(j, 1), h, :].rearrange("p a x -> p (a x)"),
                                          start=True, stop=True)
                mm.then_inc(sc, 1)

            def column_sums(src, first, last):
                for h in range(HG):
                    mm = nc.tensor.matmul(ps_z[HD * h:HD * h + HD, :], ones[:, 0:HD], src[:, h, :], start=first, stop=last)
                return mm

            def attend(n, f, stage, par, j):
                pe.wait_ge(q_copy, (n + 1) * 16)
                pe.wait_ge(q_cur, (n + 1) * 32)
                scores(0, 0, par, j)
                scores(0, 1, par, j)
                for c in range(NKC):
                    if c == NKC - 1:
                        queries(f + 1)
                    for p in range(2):
                        pe.wait_ge(ex, n * (2 * NKC) + 2 * c + p + 1)
                        if c < NKC - 1:
                            scores(c + 1, p, par, j)
                        for u in units_at.get((c, p), ()):
                            unit(u, f, stage + 1, 1 - par)
                    if c == 0:
                        pe.wait_ge(oz_cp, n * 2 + 1)
                    for h in range(HG):
                        mm = nc.tensor.matmul(ps_o[HD * h:HD * h + HD, :], vst[:, par, c, HD * h:HD * h + HD],
                                              prob[:, c % NPB, h, :], start=c == 0, stop=c == NKC - 1)
                    if c in POOL_CHUNKS:
                        mm.then_inc(pv, 1)
                    for u in units_at.get((c, 2), ()):
                        unit(u, f, stage + 1, 1 - par)
                    if c not in POOL_CHUNKS:
                        column_sums(prob[:, c % NPB], c == PE_FIRST, False).then_inc(pv, 1)
                    for u in units_at.get((c, 3), ()):
                        unit(u, f, stage + 1, 1 - par)
                maxima_to_rows(f)
                pe.wait_ge(padd, (n + 1) * NADD)
                column_sums(acc, False, True).then_inc(zdone, 1)

            def tokens(b):
                pe.wait_ge(c_par, (b + 1) * 64)
                pe.wait_ge(oz_cp, (b + 1) * (2 * NG * NQB) + 1)
                wait_alone(pe, mcp, (b + 1) * (NG * NQB) + NQB, passed)

                def step(k, par, head, tail):
                    g = b * NPAIR + k
                    a, w = tA[1 - par], tW[1 - par]

                    def output_projection(t):
                        pe.wait_ge(c_ldc[t], (g + 1) * 16)
                        if tail:
                            pe.wait_ge(c_n1, g * TPG)
                        for h in range(NG):
                            mm = nc.tensor.matmul(ps_wo[t], tC[t][:, h * P:(h + 1) * P], wo_sb[:, h, :],
                                                  start=h == 0, stop=h == NG - 1)
                        mm.then_inc(c_wo, 1)

                    if head:
                        output_projection(0)
                    if tail:
                        for t in range(TPG):
                            pe.wait_ge(c_w, (g - 1) * TPG + t + 1)
                            for c in range(IC):
                                mm = nc.tensor.transpose(ps_t[t][:, c * P:(c + 1) * P], w[t][:, c * P:(c + 1) * P], ident[:])
                            mm.then_inc(c_wt, 1)
                            pe.wait_ge(c_wtc, (g - 1) * TPG + t + 1)
                            for c in range(IC):
                                mm = nc.tensor.matmul(ps_h[t][:, c * P:(c + 1) * P], a[t][:, c * P:(c + 1) * P], hadm[:],
                                                      start=True, stop=True)
                            mm.then_inc(c_h, 1)
                    if head:
                        output_projection(1)
                    if tail:
                        for t in range(TPG):
                            pe.wait_ge(c_q, (g - 1) * TPG + t + 1)
                            for c in range(IC):
                                mm = nc.tensor.transpose(ps_t[t].bitcast(BF16)[:, c * P:(c + 1) * P],
                                                         a[t].bitcast(BF16)[:, c * P:(c + 1) * P], identb[:])
                            mm.then_inc(c_qt, 1)
                        for t in range(TPG):
                            pe.wait_ge(c_qtc, (g - 1) * TPG + t + 1)
                            for c in range(IC):
                                mm = nc.tensor.matmul(ps_h[t], w[t].bitcast(BF16)[:, c * P:(c + 1) * P], ternT[:, c, :],
                                                      start=c == 0, stop=c == IC - 1)
                            mm.then_inc(c_ffn, 1)

                pair_steps(pe, step)

            pe.wait_ge(idf, 5)
            pe.wait_ge(tern_ok, 1)
            for c in range(IC):
                for oc in range(IC):
                    nc.tensor.transpose(ps_s[:, c, :].bitcast(BF16)[:, oc * P:(oc + 1) * P],
                                        ternb[:, oc, c * P:(c + 1) * P], identb[:])
            for oc in range(IC):
                mm = nc.tensor.matmul(ps_o[:, oc * P:(oc + 1) * P], ones[:], diag[:, oc * P:(oc + 1) * P], start=True, stop=True)
            mm.then_inc(tern_t, 1)
            pe.wait_ge(mask_ld, 2 * HG * 16)
            pe.wait_ge(tern_c, 5)
            keys(0, 0, first=True)
            queries(0, first=True)
            with pe.Fori(0, NQB) as j:
                for u in range(UNITS):
                    unit(u, j, 0, 0, first=True)
                queries(j + 1)
                maxima_to_rows(j, first=True)
                wait_alone(pe, q_cur, (j + 1) * 32, passed)
            with pe.Fori(0, NB) as b:
                with pe.Fori(0, NG // 2) as half:
                    for par in range(2):
                        stage = b * NG + half * 2 + par
                        keys(stage + 1, 1 - par)
                        with pe.Fori(0, NQB) as j:
                            n = stage * NQB + j
                            attend(n, n + NQB, stage, par, j)
                tokens(b)
                wait_alone(pe, c_st, (b + 1) * (NPAIR * TPG * 16), passed)

        @block.scalar
        def _(act):
            def bias_of(which, stage):
                return bias[:, bass.ds((stage & (NG - 1)) + which * NG, 1)]

            def keys(stage, par, first=False):
                for t in range(NQB):
                    if t == 0 and not first:
                        act.wait_ge(q_stk, (stage * NQB + 1) * NSTK)
                    if t >= 2:
                        act.wait_ge(k_stk[t % 2], stage * (2 * NSTK) + NSTK)
                    wait_alone(act, kproj, stage * NQB + t + 1, passed)
                    nc.scalar.activation(hi[:, t % 2], ps_m[:, 0, :], ACT.Identity, bias=bias_of(1, stage)).then_inc(k_hi, 1)
                    act.wait_ge(vproj, stage * NQB + t + 1)
                    nc.scalar.activation(vst[:, par, t * (QB // P):(t + 1) * (QB // P), :].rearrange("p c d -> p (c d)"),
                                         ps_m[:, 1, :], ACT.Copy).then_inc(v_cp, 1)

            def queries(f):
                wait_alone(act, qproj, f + 1, passed)
                nc.scalar.activation(hi[:, 0], ps_m[:, 0, :], ACT.Identity, bias=bias_of(0, f >> 2)).then_inc(q_hi, 1)

            def maxima_rows(f):
                act.wait_ge(mtr, f + 1)
                nc.scalar.activation(mrow[:], ps_m[0:2 * HG * NQB, 1, 0:P], ACT.Copy).then_inc(mcp, 1)

            def attend(n, f):
                for c in range(NKC):
                    for p in range(2):
                        act.wait_ge(sc, n * (2 * NKC) + 2 * c + p + 1)
                        if c >= NPB and p == 0:
                            act.wait_ge(pv, n * NKC + c - NPB + 1)
                            if c - NPB in POOL_CHUNKS:
                                act.wait_ge(padd, n * NADD + ADD_OF[c - NPB] + 1)
                        if c == (NKC - 1) % NPB and p == 1:
                            act.wait_ge(cst, (n + 1) * 16)
                        nc.scalar.activation(prob[:, c % NPB, 2 * p:2 * p + 2, :], ps_s[:, 2 * p:2 * p + 2, :],
                                             ACT.Exp, scale=SCALE).then_inc(ex, 1)
                queries(f + 1)
                act.wait_ge(pv, (n + 1) * NKC)
                nc.scalar.activation(obuf, ps_o[:], ACT.Copy).then_inc(oz_cp, 1)
                maxima_rows(f)
                act.wait_ge(zdone, n + 1)
                nc.scalar.activation(zbuf, ps_z[:], ACT.Copy).then_inc(oz_cp, 1)

            def tokens(b):
                def step(k, par, head, tail):
                    g = b * NPAIR + k
                    a, w = tA[1 - par], tW[1 - par]
                    former = (g - 1) * TPG
                    chain = b * CHAINS + k * 2

                    def roots(number, cols):
                        act.wait_ge(c_ve, number)
                        nc.scalar.activation(lnv[:, cols, 1], lnv[:, cols, 0], ACT.Sqrt).then_inc(c_sd, 1)

                    if tail:
                        for t in range(TPG):
                            if not head:
                                act.wait_ge(c_st, (former - TPG) * 16)
                            act.wait_ge(c_wt, former + t + 1)
                            nc.scalar.activation(a[t], ps_t[t], ACT.Copy).then_inc(c_wtc, 1)
                        for t in range(TPG):
                            act.wait_ge(c_q1, former + t + 1)
                            act.wait_ge(c_h, former + t + 1)
                            nc.scalar.activation(a[t].bitcast(BF16)[:, 0:D], w[t], ACT.Copy, bias=-MAGIC).then_inc(c_q, 1)
                    if head:
                        roots(chain + 1, slice(0, TPG))
                    if tail:
                        for t in range(TPG):
                            act.wait_ge(c_qt, former + t + 1)
                            act.wait_ge(c_q, former + t + 1)
                            nc.scalar.activation(w[t].bitcast(BF16)[:, 0:D], ps_t[t].bitcast(BF16)[:, 0:D],
                                                 ACT.Copy).then_inc(c_qtc, 1)
                    roots(chain + 1 + head, slice(0 if head else TPG, 2 * TPG if tail else TPG))

                pair_steps(act, step)

            act.sem_inc(oz_cp, 1)
            act.wait_ge(band_mx, 1)
            nc.scalar.activation(band_e, band_row, ACT.Exp, bias=band_s[:, 0:1], accum_out=band_s[:, 1:2]).then_inc(band_ex, 1)
            act.wait_ge(bias_ld, 16)
            keys(0, 0, first=True)
            act.wait_ge(k_stk[0], 2 * NSTK)
            queries(0)
            with act.Fori(0, NQB) as j:
                queries(j + 1)
                maxima_rows(j)
            with act.Fori(0, NB) as b:
                with act.Fori(0, NG // 2) as half:
                    for par in range(2):
                        stage = b * NG + half * 2 + par
                        keys(stage + 1, 1 - par)
                        with act.Fori(0, NQB) as j:
                            n = stage * NQB + j
                            attend(n, n + NQB)
                tokens(b)
                wait_alone(act, c_st, (b + 1) * (NPAIR * TPG * 16), passed)

        @block.vector
        def _(dve):
            def bias_of(which, stage):
                return bias[:, bass.ds((stage & (NG - 1)) + which * NG, 1)]

            def low_part(dst, high, which, stage):
                return nc.vector.scalar_tensor_tensor(out=dst, in0=ps_m[:, 0, :], scalar=bias_of(which, stage),
                                                      in1=high.bitcast(F32), op0=ALU.add, op1=ALU.subtract)

            def keys(stage, first=False):
                for t in range(NQB):
                    if t == 0 and not first:
                        dve.wait_ge(q_stk, (stage * NQB + 1) * NSTK)
                    dve.wait_ge(k_hi, stage * NQB + t + 1)
                    if t >= 2:
                        dve.wait_ge(k_stk[t % 2], stage * (2 * NSTK) + NSTK)
                    low_part(lo[:, t % 2], hi[:, t % 2], 1, stage).then_inc(k_lo, 1)

            def queries(f):
                dve.wait_ge(q_hi, f + 1)
                low_part(lo[:, 0], hi[:, 0], 0, f >> 2).then_inc(q_lo, 1)

            def maxima(f):
                for u in range(UNITS):
                    dve.wait_ge(msc, f * UNITS + u + 1)
                    m, kb = divmod(u, NQB)
                    nc.vector.tensor_reduce(umax[:, m, kb:kb + 1], ps_m[:, u % 2, :], AX.X, ALU.max).then_inc(mred, 1)
                dve.wait_ge(mred, (f + 1) * UNITS)
                nc.vector.tensor_reduce(negm[:], umax[:], AX.X, ALU.max, negate=True).then_inc(mstep, 1)
                dve.wait_ge(mstep, f * 2 + 1)
                nc.vector.tensor_copy(mhi[:], negm[:]).then_inc(mstep, 1)
                dve.wait_ge(mstep, f * 2 + 2)
                nc.vector.tensor_copy(msplit[:, 0:HG * NQB], mhi[:].bitcast(F32))
                nc.vector.tensor_tensor(msplit[:, HG * NQB:], negm[:], mhi[:].bitcast(F32), ALU.subtract).then_inc(mneg, 1)

            def normalise(n, stage):
                dve.wait_ge(oz_cp, n * 2 + 3)
                nc.vector.reciprocal(zbuf, zbuf).then_inc(zinv, 1)
                dve.wait_ge(zinv, n + 1)
                nc.vector.tensor_tensor(obuf, obuf, zbuf, ALU.mult).then_inc(cnorm, 1)
                dve.wait_ge(cnorm, n + 1)
                nc.vector.tensor_scalar(obuf, obuf, bias_of(2, stage), None, ALU.add).then_inc(cbias, 1)

            def tokens(b):
                wait_alone(dve, c_par, (b + 1) * 64, passed)

                def step(k, par, head, tail):
                    g = b * NPAIR + k
                    former = (g - 1) * TPG
                    r, r0, w0, a0 = tR[par], tR[1 - par], tW[1 - par], tA[1 - par]
                    chain = b * CHAINS + k * 2
                    base = b * D_BATCH + (D_FIRST - D_BOTH + k * D_BOTH if tail else 0)
                    steps = [0]

                    def mark(ins):
                        steps[0] += 1
                        ins.then_inc(c_dve, 1)
                        return steps[0]

                    def own(k):
                        dve.wait_ge(c_dve, base + k)

                    def statistics(col, src):
                        k = mark(nc.vector.bn_stats(stats[:, col, :], src))
                        wait_alone(dve, c_dve, base + k, passed)
                        return mark(nc.vector.bn_aggr(mv[:, col, :], stats[:, col, :]))

                    def inverse_roots(last, number, cols):
                        own(last)
                        nc.vector.tensor_scalar(lnv[:, cols, 0], mv[:, cols, 1], LN_EPS, None, ALU.add).then_inc(c_ve, 1)
                        dve.wait_ge(c_sd, number)
                        v, s, r, w = (lnv[:, cols, i] for i in range(4))
                        own(mark(nc.vector.reciprocal(r, s)))
                        own(mark(nc.vector.tensor_tensor(w, r, r, ALU.mult)))
                        own(mark(nc.vector.tensor_tensor(w, w, v, ALU.mult)))
                        own(mark(nc.vector.tensor_scalar(w, w, -0.5, 1.5, ALU.mult, ALU.add)))
                        own(mark(nc.vector.tensor_tensor(r, r, w, ALU.mult)))

                    def normal(col, buf):
                        return nc.vector.tensor_scalar(buf, buf, mv[:, col, 0:1], lnv[:, col, 2:3], ALU.subtract, ALU.mult)

                    def attention_sum(t):
                        dve.wait_ge(c_wo, g * TPG + t + 1)
                        dve.wait_ge(c_xb, g * TPG + t + 1)
                        own(mark(nc.vector.tensor_tensor(r[t], ps_wo[t], r[t], ALU.add)))
                        return statistics(t, r[t])

                    if head and not tail:
                        attention_sum(0)
                    if tail:
                        for t in range(TPG):
                            if t == 1 and head:
                                attention_sum(0)
                            dve.wait_ge(c_h, former + t + 1)
                            last = mark(nc.vector.tensor_reduce(qsc[:, t, 0:1], ps_h[t], AX.X, ALU.max,
                                                                apply_absolute_value=True))
                        own(last)
                        own(mark(nc.vector.tensor_scalar(qsc[:, :, 1], qsc[:, :, 0], 1e-5, 1.0 / 7.0, ALU.max, ALU.mult)))
                        own(mark(nc.vector.reciprocal(qsc[:, :, 2], qsc[:, :, 1])))
                        for t in range(TPG):
                            own(mark(nc.vector.tensor_scalar(w0[t], ps_h[t], qsc[:, t, 2:3], 7.0, ALU.mult, ALU.min)))
                            nc.vector.tensor_scalar(w0[t], w0[t], -8.0, MAGIC, ALU.max, ALU.add).then_inc(c_q1, 1)
                    if head:
                        last = attention_sum(1)
                        inverse_roots(last, chain + 1, slice(0, TPG))
                        for t in range(TPG):
                            normal(t, r[t]).then_inc(c_n1, 1)
                    if tail:
                        for t in range(TPG):
                            dve.wait_ge(c_ffn, former + t + 1)
                            own(mark(nc.vector.scalar_tensor_tensor(out=a0[t], in0=ps_h[t], scalar=qsc[:, t, 1:2],
                                                                    in1=wscale[:], op0=ALU.mult, op1=ALU.mult)))
                            own(mark(nc.vector.tensor_tensor(a0[t], a0[t], r0[t], ALU.add)))
                            last = statistics(TPG + t, a0[t])
                    if head:
                        for t in range(TPG):
                            dve.wait_ge(c_ng, g * TPG + t + 1)
                            own(mark(nc.vector.tensor_tensor(r[t], r[t], tS[t], ALU.add)))
                            last = statistics(t, r[t])
                    inverse_roots(last, chain + 1 + head, slice(0 if head else TPG, 2 * TPG if tail else TPG))
                    if head:
                        for t in range(TPG):
                            normal(t, r[t]).then_inc(c_x1, 1)
                        for t in range(TPG):
                            dve.wait_ge(c_x1, g * TPG + t + 1)
                            a, s, half = r[t], tS[t], D // 2
                            mark(nc.vector.tensor_tensor(s[:, 0:half], a[:, 0:half], a[:, half:], ALU.add))
                            own(mark(nc.vector.tensor_tensor(s[:, half:], a[:, 0:half], a[:, half:], ALU.subtract)))
                            sv = s.rearrange("p (a b n) -> p a b n", a=2, b=2)
                            wv = tW[par][t].rearrange("p (a b n) -> p a b n", a=2, b=2)
                            mark(nc.vector.tensor_tensor(wv[:, :, 0, :], sv[:, :, 0, :], sv[:, :, 1, :], ALU.add))
                            nc.vector.tensor_tensor(wv[:, :, 1, :], sv[:, :, 0, :], sv[:, :, 1, :], ALU.subtract)\
                                .then_inc(c_w, 1)
                    if tail:
                        for t in range(TPG):
                            normal(TPG + t, a0[t]).then_inc(c_o, 1)
                    assert steps[0] == (D_BOTH if head and tail else D_FIRST if head else D_LAST), steps[0]

                pair_steps(dve, step)

            done = [0]

            def step(ins):
                done[0] += 1
                ins.then_inc(dstep, 1)
                dve.wait_ge(dstep, done[0])

            dve.wait_ge(band_ld, 16)
            nc.vector.tensor_reduce(band_s[:, 0:1], band_row, AX.X, ALU.max, negate=True).then_inc(band_mx, 1)
            step(nc.vector.memset(band_e_pad, PAD))
            dve.wait_ge(band_ex, 1)
            step(nc.vector.reciprocal(band_s[:, 2:3], band_s[:, 1:2]))
            step(nc.vector.tensor_scalar(band_e, band_e, band_s[:, 2:3], None, ALU.mult))
            step(nc.vector.max(band_s[:, 8:16], band_all))
            step(nc.vector.memset(band_s[:, 8 + TOPK:16], PAD))
            step(nc.vector.match_replace(out=band_all2, in_to_replace=band_s[:, 8:16], in_values=band_all, imm_value=FOUND))
            nc.vector.tensor_scalar(qmask[:, 0:LBAND], band_all2[:, 0:LBAND], FOUND, MASKED, ALU.is_equal, ALU.mult)\
                .then_inc(mask_ok, 1)
            dve.wait_ge(wf_ld, 16)
            step(nc.vector.tensor_reduce(small[:, 0:IC], wf, AX.X, ALU.add, apply_absolute_value=True))
            step(nc.vector.tensor_scalar(small[:, 0:IC], small[:, 0:IC], 1.0 / D, 1e-5, ALU.mult, ALU.max))
            step(nc.vector.tensor_scalar(small[:, 4:4 + IC], small[:, 0:IC], 0.5, None, ALU.mult))
            step(nc.vector.tensor_scalar(small[:, 8:8 + IC], small[:, 0:IC], -0.5, None, ALU.mult))
            dve.wait_ge(idf, 5)
            for oc in range(IC):
                step(nc.vector.tensor_scalar(neg, wf[:, oc], small[:, 8 + oc:9 + oc], None, ALU.is_lt))
                step(nc.vector.scalar_tensor_tensor(out=ternb[:, oc], in0=wf[:, oc], scalar=small[:, 4 + oc:5 + oc], in1=neg,
                                                    op0=ALU.is_gt, op1=ALU.subtract))
                ins = nc.vector.tensor_scalar(diag[:, oc * P:(oc + 1) * P], ident[:], small[:, oc:oc + 1], None, ALU.mult)
                if oc < IC - 1:
                    step(ins)
            ins.then_inc(tern_ok, 1)
            dve.wait_ge(tern_t, 1)
            for c in range(IC):
                nc.vector.tensor_copy(ternT[:, c, :], ps_s[:, c, :].bitcast(BF16)[:, 0:D]).then_inc(tern_c, 1)
            nc.vector.tensor_copy(wscale[:], ps_o[:]).then_inc(tern_c, 1)
            dve.wait_ge(bias_ld, 16)
            keys(0, first=True)
            queries(0)
            with dve.Fori(0, NQB) as j:
                maxima(j)
                queries(j + 1)
            with dve.Fori(0, NB) as b:
                with dve.Fori(0, NG // 2) as half:
                    for par in range(2):
                        stage = b * NG + half * 2 + par
                        keys(stage + 1)
                        with dve.Fori(0, NQB) as j:
                            n = stage * NQB + j
                            maxima(n + NQB)
                            queries(n + (NQB + 1))
                            normalise(n, stage)
                tokens(b)
                wait_alone(dve, c_st, (b + 1) * (NPAIR * TPG * 16), passed)

        @block.gpsimd
        def _(pool):
            def attend(n):
                for i in range(NADD):
                    c = POOL_CHUNKS[i + 1]
                    pool.wait_ge(ex, n * (2 * NKC) + 2 * c + 2)
                    if i == 0:
                        a = prob[:, POOL_CHUNKS[0] % NPB]
                    else:
                        pool.wait_ge(padd, n * NADD + i)
                        a = acc[:]
                    nc.gpsimd.tensor_tensor(acc[:], a, prob[:, c % NPB], ALU.add).then_inc(padd, 1)

            def tokens(b):
                wait_alone(pool, c_par, (b + 1) * 64, passed)

                def add_bias(k, t, par):
                    pool.wait_ge(c_ldx[t], (b * NPAIR + k + 1) * 16)
                    nc.gpsimd.tensor_tensor(tR[par][t], tX[t], bob, ALU.add).then_inc(c_xb, 1)

                def add_beta(k, t):
                    pool.wait_ge(c_xb, (b * NPAIR + k) * TPG + t + 1)
                    nc.gpsimd.tensor_tensor(tS[t], tX[t], bet, ALU.add).then_inc(c_xg, 1)

                def step(k, par, more=True):
                    g = b * NPAIR + k
                    for t in range(TPG):
                        pool.wait_ge(c_n1, g * TPG + t + 1)
                        pool.wait_ge(c_xg, g * TPG + t + 1)
                        nc.gpsimd.tensor_tensor(tR[par][t], tR[par][t], gam, ALU.mult).then_inc(c_ng, 1)
                    if more:
                        for t in range(TPG):
                            pool.wait_ge(c_x1, g * TPG + t + 1)
                            add_bias(k + 1, t, 1 - par)
                        for t in range(TPG):
                            pool.wait_ge(c_w, g * TPG + t + 1)
                            add_beta(k + 1, t)

                for t in range(TPG):
                    add_bias(0, t, 0)
                for t in range(TPG):
                    add_beta(0, t)
                step(0, 0)
                with pool.Fori(0, (NPAIR - 2) // 2) as i:
                    step(i * 2 + 1, 1)
                    step(i * 2 + 2, 0)
                step(NPAIR - 1, 1, more=False)

            nc.gpsimd.memset(ones[:], 1.0).then_inc(idf, 1)
            pool.wait_ge(idf, 1)
            nc.gpsimd.memset(ident[:], 0.0).then_inc(idf, 1)
            pool.wait_ge(idf, 2)
            nc.gpsimd.affine_select(out=ident[:], in_=ident[:], compare_op=ALU.not_equal, fill=1.0, base=0,
                                    pattern=[[-1, P]], channel_multiplier=1).then_inc(idf, 2)
            pool.wait_ge(idf, 4)
            nc.gpsimd.tensor_copy(identb[:], ident[:]).then_inc(idf, 1)
            pool.wait_ge(idf, 5)
            nc.gpsimd.memset(qmask[:, LBAND:].bitcast(F32), 0.0).then_inc(mask_ok, 1)
            nc.gpsimd.memset(qcur[RMASK:RALL].bitcast(F32), 1.0).then_inc(stk_ones, 1)
            pool.wait_ge(stk_ones, 1)
            nc.gpsimd.memset(qnew[RMASK:RSTACK].bitcast(F32), 1.0).then_inc(stk_ones, 1)
            for i in range(2):
                pool.wait_ge(stk_ones, 2 + i)
                nc.gpsimd.memset(kst[i][RMASK:RALL].bitcast(F32), 1.0).then_inc(stk_ones, 1)
            pool.wait_ge(stk_ones, 4)
            pool.wait_ge(mask_ok, 2)
            with pool.Fori(0, NB) as b:
                with pool.Fori(0, NG) as g:
                    stage = b * NG + g
                    with pool.Fori(0, NQB) as j:
                        attend(stage * NQB + j)
                tokens(b)
                wait_alone(pool, c_st, (b + 1) * (NPAIR * TPG * 16), passed)


def kernel(L0_attn_x, L0_attn_band_importance, L0_attn_Wq, L0_attn_bq, L0_attn_Wk, L0_attn_bk, L0_attn_Wv, L0_attn_bv,
           L0_attn_Wo, L0_attn_bo, L0_attn_gamma, L0_attn_beta, L0_ffn_weight):
    import concourse.bacc as bacc
    from concourse.bass_utils import run_bass_kernel_spmd

    nc = bacc.Bacc("TRN2", target_bir_lowering=False, num_devices=1)
    x = np.asarray(L0_attn_x).reshape(NB * L, D)
    h = np.ones((1, 1), np.float32)
    while h.shape[0] < P:
        h = np.block([[h, h], [h, -h]])

    def interleave(a):
        return a.reshape(-1, NG, HG, HD).transpose(0, 1, 3, 2).reshape(a.shape)

    wq, wk, wv = (np.asarray(w).T for w in (L0_attn_Wq, L0_attn_Wk, L0_attn_Wv))
    bq, bk, bv = (np.asarray(v) for v in (L0_attn_bq, L0_attn_bk, L0_attn_bv))
    arrays = {
        "x": x,
        "xT": x.T,
        "wT": np.stack([interleave(wq), interleave(wk), wv]),
        "bqkv": np.stack([v.reshape(NG, P).T for v in (interleave(bq), interleave(bk), bv)], 1).reshape(P, 3 * NG),
        "woT": np.asarray(L0_attn_Wo).T,
        "w_ffn": L0_ffn_weight,
        "band": L0_attn_band_importance,
        "gamma": L0_attn_gamma,
        "beta": L0_attn_beta,
        "bo": L0_attn_bo,
        "had": (h / np.sqrt(D)).astype(np.float32),
    }
    arrays = {f"in_{k}_dram": np.ascontiguousarray(v) for k, v in arrays.items()}
    args = [nc.dram_tensor(k, v.shape, mybir.dt.from_np(v.dtype), kind="ExternalInput").ap() for k, v in arrays.items()]
    out = nc.dram_tensor("out_dram", (NB * L, D), F32, kind="ExternalOutput").ap()
    build(nc, *args, out)
    r = run_bass_kernel_spmd(nc, [arrays], core_ids=[0])
    return r.results[0]["out_dram"].reshape(NB, L, D)
```
